# Optimizing a Trainium2 kernel written in Bass

```python
import numpy as np
import jax
import jax.numpy as jnp

def _softmax(x, axis=-1):
    return jax.nn.softmax(x, axis=axis)
def _gelu(x):
    return jax.nn.gelu(x, approximate=True)
def _silu(x):
    return jax.nn.silu(x)
def _sigmoid(x):
    return jax.nn.sigmoid(x)
def _layernorm(x, axis=-1, eps=1e-5):
    m = jnp.mean(x, axis=axis, keepdims=True)
    v = jnp.var(x, axis=axis, keepdims=True)
    return (x - m) / jnp.sqrt(v + eps)
def _scatter_add(tgt, idx, src, axis=0):
    return tgt.at[idx].add(src)
def _segment_sum(src, seg, n):
    return jax.ops.segment_sum(src, seg, n)

kernel_name = 'mk_adj_preln_d2_adj_64_d6db37'

def setup_inputs(seed: int = 0):
    np.random.seed(seed)
    _w = jnp.asarray
    def _rec_inputs():
        import jax
        import jax.numpy as jnp
        _gk = jax.random.key(seed)
        x = -0.0005207 + 1.001 * jax.random.normal(jax.random.fold_in(_gk, 1), (16, 1024, 64), jnp.float32)
        _w = (1.0 + jnp.arange(1024, dtype=jnp.float32)) ** -0.5
        _w = _w / _w.mean()
        _pij = jnp.clip(0.00390625 * _w[:, None] * _w[None, :], 0.0, 1.0)
        _a = jax.random.uniform(jax.random.fold_in(_gk, 2), (16, 1024, 1024)) < _pij
        _a = jnp.logical_or(_a, jnp.eye(1024, dtype=bool))
        _af = _a.astype(jnp.float32)
        _af = _af * jax.random.uniform(jax.random.fold_in(_gk, 3), (16, 1024, 1024), jnp.float32, 0.05, 1)
        adj = _af
        _nm = jnp.ones((16, 1024), dtype=bool)
        nodemask = _nm
        return x, adj, nodemask
    x, adj, nodemask = _rec_inputs()
    def _L0_gnn_setup():
        import jax, jax.numpy as jnp
        import numpy as np
        key = jax.random.key(seed)
        k1, k2 = jax.random.split(key)
        B, N, D = (8, 4096, 64)
        x = jax.random.normal(k1, (B, N, D), dtype=jnp.float32)
        A = jax.random.uniform(k2, (B, N, N), dtype=jnp.float32)
        return {'x': x, 'A': A}
    _L0_gnn_all = _L0_gnn_setup()
    _L0_gnn_in = {k: v for k, v in _L0_gnn_all.items() if k in ()}
    del _L0_gnn_all

    def _L1_gnn_setup():
        import jax, jax.numpy as jnp
        import numpy as np
        B, N, C, H = (8, 512, 64, 128)
        T, K = (10, 2)
        TAUS = (0.25, 0.5, 0.75)
        WTS = (0.25, 0.5, 0.25)
        EPS_GIN = 0.0
        AVG_DEG = 32.0
        key = jax.random.key(seed)
        ks = jax.random.split(key, 6)
        x = jax.random.normal(ks[0], (B, N, C), jnp.float32)
        u = jax.random.uniform(ks[1], (B, N, N))
        a = u < AVG_DEG / N
        adj = jnp.maximum(a, jnp.swapaxes(a, 1, 2)).astype(jnp.float32)
        mask = jax.random.bernoulli(ks[2], 0.9, (B, N))
        W1 = jax.random.normal(ks[3], (C, H), jnp.float32) / np.float32(np.sqrt(C))
        b1 = jnp.zeros((H,), jnp.float32)
        W2 = jax.random.normal(ks[4], (H, C), jnp.float32) / np.float32(np.sqrt(H))
        b2 = jnp.zeros((C,), jnp.float32)
        return {'x': x, 'adj': adj, 'mask': mask, 'W1': W1, 'b1': b1, 'W2': W2, 'b2': b2}
    _L1_gnn_all = _L1_gnn_setup()
    _L1_gnn_in = {k: v for k, v in _L1_gnn_all.items() if k in ('W1', 'b1', 'W2', 'b2', )}
    del _L1_gnn_all

    return {
        "x": x,
        "adj": adj,
        "nodemask": nodemask,
        "L1_gnn_W1": _L1_gnn_in["W1"],
        "L1_gnn_b1": _L1_gnn_in["b1"],
        "L1_gnn_W2": _L1_gnn_in["W2"],
        "L1_gnn_b2": _L1_gnn_in["b2"],
    }

def reference(x, adj, nodemask, L1_gnn_W1, L1_gnn_b1, L1_gnn_W2, L1_gnn_b2):
    import jax
    import jax.numpy as jnp
    def _L0_gnn_ref(x, A):
        import jax, jax.numpy as jnp
        import numpy as np
        deg = jnp.clip(jnp.sum(A, axis=2, keepdims=True), 1.0, None)
        A_norm = A / deg
        messages = jnp.matmul(A_norm, x)
        return messages

    def _L1_gnn_ref(x, adj, mask, W1, b1, W2, b2):
        import jax, jax.numpy as jnp
        import numpy as np
        B, N, C, H = (8, 512, 64, 128)
        T, K = (10, 2)
        TAUS = (0.25, 0.5, 0.75)
        WTS = (0.25, 0.5, 0.25)
        EPS_GIN = 0.0
        AVG_DEG = 32.0
        Bc, Nc, Cc = x.shape
        eye = jnp.eye(Nc, dtype=bool)
        adj_ = jnp.where(eye, 1.0, adj)
        neigh = (adj_ > 0) & ~eye
        ni = neigh.astype(jnp.int32)
        rank = jnp.cumsum(ni, axis=-1) - ni
        nb = ni.sum(-1)
        skip = jnp.where(nb > T, (nb + K - 1) // K, 1)
        skip = jnp.maximum(skip, 1)
        sk = skip[:, :, None]
        rem = neigh & (sk > 1) & (rank % sk == sk - 1) & mask[:, :, None]
        rem = rem | jnp.swapaxes(rem, 1, 2)
        adj_d = jnp.where(rem, 0.0, adj_)
        nd = adj_d > 0
        vals = jnp.where(nd[..., None], x[:, None, :, :], jnp.inf)
        s = jnp.sort(vals, axis=2)
        nv = nd.sum(2)
        agg = jnp.zeros_like(x)
        for tau, w in zip(TAUS, WTS):
            pos = jnp.asarray(tau, x.dtype) * jnp.maximum(nv - 1, 0).astype(x.dtype)
            lo = jnp.floor(pos).astype(jnp.int32)
            hi = jnp.ceil(pos).astype(jnp.int32)
            frac = (pos - lo.astype(x.dtype))[..., None]
            idx_lo = jnp.broadcast_to(lo[:, :, None, None], (Bc, Nc, 1, Cc))
            idx_hi = jnp.broadcast_to(hi[:, :, None, None], (Bc, Nc, 1, Cc))
            v_lo = jnp.take_along_axis(s, idx_lo, axis=2)[:, :, 0, :]
            v_hi = jnp.take_along_axis(s, idx_hi, axis=2)[:, :, 0, :]
            agg = agg + jnp.asarray(w, x.dtype) * (v_lo + frac * (v_hi - v_lo))
        agg = jnp.where(nv[..., None] > 0, agg, 0.0)
        out = (1.0 + EPS_GIN) * x + agg
        h = jax.nn.relu(out @ W1 + b1)
        y = h @ W2 + b2
        return y * mask[..., None].astype(y.dtype)

    h = jnp.maximum(_layernorm(x, axis=-1), 0.0)
    x = x + _L0_gnn_ref(h, adj)
    h = jnp.maximum(_layernorm(x, axis=-1), 0.0)
    x = x + _L1_gnn_ref(h, adj, nodemask, L1_gnn_W1, L1_gnn_b1, L1_gnn_W2, L1_gnn_b2)
    return x


_drawn_inputs = setup_inputs


def setup_inputs(seed=0):
    import zlib

    import numpy as np

    out = dict(_drawn_inputs(seed))
    spreads = {'L1_gnn_b1': (0.0, 0.1), 'L1_gnn_b2': (0.0, 0.1)}
    factors = {}
    for name, (base, spread) in spreads.items():
        noise = np.random.default_rng([zlib.crc32(name.encode()), seed]).standard_normal(out[name].shape)
        drawn = base * np.exp(spread * noise) if base else spread * noise
        out[name] = jnp.asarray(drawn.astype(out[name].dtype))
    for name, factor in factors.items():
        out[name] = (out[name] * factor).astype(out[name].dtype)
    return out
```

```python
from contextlib import ExitStack

import concourse.bass as bass
from concourse import mybir

ALU = mybir.AluOpType
ACT = mybir.ActivationFunctionType
F32 = mybir.dt.float32
F16 = mybir.dt.float16
I32 = mybir.dt.int32
AX = mybir.AxisListType.X

B, N, C, H = 16, 1024, 64, 128
P = 128
T = N // P
NP = B // 2
TAUS = (0.25, 0.5, 0.75)
WTS = (0.25, 0.5, 0.25)
HSCALE = 4096.0
PAD = 65536.0
BIG = 1.0e9
NOMATCH = 9999.0

CLASSES = [(0, 8, 128), (8, 80, 32), (80, 256, 16), (256, 1024, 12)]
NET12 = [
    [(0, 8), (1, 7), (2, 6), (3, 11), (4, 10), (5, 9)],
    [(0, 1), (2, 5), (3, 4), (6, 9), (7, 8), (10, 11)],
    [(0, 2), (1, 6), (5, 10), (9, 11)],
    [(0, 3), (1, 2), (4, 6), (5, 7), (8, 11), (9, 10)],
    [(1, 4), (3, 5), (6, 8), (7, 10)],
    [(1, 3), (2, 5), (6, 9), (8, 10)],
    [(2, 3), (4, 5), (6, 7), (8, 9)],
    [(4, 6), (5, 7)],
    [(3, 4), (5, 6), (7, 8)],
]

CF_ID, CF_BIASQ, CF_WQ, CF_EPS, CF_CAP, CF_ONE, CF_N = 0, 128, 131, 134, 135, 139, 267
(CH_ID, CH_NEG, CH_PRE, CH_ONE, CH_OFF, CH_IOTA, CH_SEL) = range(7)


class Token:

    def __init__(self, lane):
        self.lane, self.used, self.value = lane, False, None


class DmaToken:
    def __init__(self, sem, value):
        self.sem, self.value, self.used = sem, value, True


class Lane:

    def __init__(self, sem):
        self.sem, self.ops = sem, []

    def do(self, fn, *waits):
        t = Token(self)
        for w in waits:
            if w is not None:
                w.used = True
        self.ops.append((fn, [w for w in waits if w is not None], t))
        return t

    def count(self):
        n = 0
        for _, _, t in self.ops:
            if t.used:
                n += 1
                t.value = n

    def issue(self, eng):
        seen = {}
        for fn, waits, t in self.ops:
            for w in waits:
                sem = w.sem if isinstance(w, DmaToken) else w.lane.sem
                if seen.get(id(sem), 0) < w.value:
                    eng.wait_ge(sem, w.value)
                    seen[id(sem)] = w.value
            ins = fn(eng)
            if t.used:
                ins.then_inc(self.sem, 1)


def merge_stages(n):
    p = 1
    while p < n:
        k = p
        while k >= 1:
            yield p, k
            k //= 2
        p *= 2


def stage_views(x, p, k):
    if k == p:
        v = x.rearrange("q (b h p) n -> q b h (p n)", h=2, p=p)
        return v[:, :, 0, :], v[:, :, 1, :], None
    c = 2 * p // k
    v = x.rearrange("q (b c k) n -> q b c (k n)", c=c, k=k)
    return v[:, :, 1:c - 1:2, :], v[:, :, 2:c:2, :], v[:, :, 0:c:c - 1, :]


def program(nc, x_d, adj_d, mask_d, w1_d, b1_d, w2_d, b2_d, cf_d, ch_d, out_d):
    with ExitStack() as ctx:
        def sb(name, shape, dt=F32):
            return ctx.enter_context(nc.sbuf_tensor(name, shape, dt))

        def sem(name):
            return ctx.enter_context(nc.semaphore(name))

        banks = {k: ctx.enter_context(nc.psum_tensor("ps" + k, [P, 512], F32))
                 for k in ("T0", "T1", "L", "S0", "S1", "G0", "G1", "M")}

        X = sb("X", [P, 2, 2, T, C])
        H0A = sb("H0A", [P, 2 * T, C + 1])
        XC = sb("XC", [P, 2 * T, C])
        H1 = sb("H1", [P, T, 2, C])
        HL = sb("HL", [P, 2, 2, T, C], F16)
        NADJ = 4
        ADJ = sb("ADJ", [P, NADJ, N])
        ADJT = sb("ADJT", [P, 2, 4, P])
        OHB = sb("OHB", [P, 16384], F16)
        NEI = OHB[:, 0:8192]
        CUM = OHB[:, 8192:16384]
        POS = sb("POS", [P, 2, T, N], F16)
        NSL = 16
        SL = sb("SL", [P, NSL, 768])
        SA = sb("SA", [P, 16 * 176])
        SB = sb("SB", [P, 16 * 176])
        RED = sb("RED", [P, 256])
        NVN = sb("NVN", [P, N])
        COEF = sb("COEF", [P, 2, N], F16)
        RQ = sb("RQ", [P, 3, 512], F16)
        H1T = sb("H1T", [P, N])
        ZF = sb("ZF", [P, N])
        FL = sb("FL", [1, 2, N], F16)
        ANY = sb("ANY", [1, NP])
        CF = sb("CF", [P, CF_N])
        CH = sb("CH", [P, 7, P], F16)
        W1 = sb("W1", [P, H])
        W2 = sb("W2", [P, C])
        B1 = sb("B1", [P, 1])
        B2 = sb("B2", [1, C])
        MU8 = sb("MU8", [P, P], mybir.dt.uint8)
        MKF = SL[:, 0, 0:128]
        MK = sb("MK", [P, B * T])
        ST = sb("ST", [P, 6, 2 * T])
        SK = sb("SK", [P, 8, T])
        FB = sb("FB", [P, 4])
        COL = sb("COL", [P, 2, T, 1], F16)

        s = {k: sem("s_" + k) for k in ("pe", "act", "dve", "pool", "sp")}
        PE, AC, DV, PO, SP = (Lane(s[k]) for k in ("pe", "act", "dve", "pool", "sp"))
        s_adj = [sem(f"s_adj{i}") for i in range(NADJ)]
        s_x = [sem(f"s_x{i}") for i in range(2)]
        s_out = [sem(f"s_out{i}") for i in range(2)]
        s_c = sem("s_c")
        f_p, f_d, f_l = sem("f_p"), sem("f_d"), sem("f_l")

        idf = CF[:, CF_ID:CF_ID + P]

        def dma(dst, src, sm, value, *waits):
            SP.do(lambda e: Done(e.dma_start(dst, src).then_inc(sm, 16)), *waits)
            return DmaToken(sm, value)

        class Done:

            def __init__(self, ins):
                self.ins = ins

        n_c = 0

        def const(dst, src):
            nonlocal n_c
            n_c += 16
            return dma(dst, src, s_c, n_c)

        const(CF[:, :], cf_d)
        const(CH[:, :, :], ch_d)
        const(W1[0:C, :], w1_d)
        const(W1[C:P, :], w1_d)
        const(W2[:, :], w2_d)
        const(B1[:, :], b1_d.rearrange("(h o) -> h o", o=1))
        const(B2[:, :], b2_d.rearrange("(o c) -> o c", o=1))
        c_all = const(MU8[:, :], mask_d.rearrange("b (t p) -> (b t) p", p=P))
        t_one = DV.do(lambda e: e.memset(H0A[:, :, C:C + 1], 1.0))
        t_zf = DV.do(lambda e: e.memset(ZF[:, :], 0.0))
        t = DV.do(lambda e: e.tensor_copy(MKF, MU8[:, :]), c_all)
        t = PE.do(lambda e: e.transpose(banks["M"][:, 0:P], MKF, idf), t, c_all)
        t_mk = DV.do(lambda e: e.tensor_copy(MK[:, :], banks["M"][:, 0:P]), t)
        free = {k: None for k in banks}
        free["M"] = t_mk

        adj_n, adj_free = 0, [None] * NADJ
        at_free = [None, None]
        st = {"T": 0, "S": 0, "G": 0, "AT": 0}

        def ring(kind):
            k = f"{kind}{st[kind] % 2}"
            st[kind] += 1
            return k

        tok = {}
        oh_free = [None, None]
        pending = {}
        x_ready, x_free = {}, {0: None, 1: None}
        out_n = [0, 0]

        def layernorm_relu(src, outs, waits, tag):
            sums, mean, var, sd, rs = (ST[:, i, :] for i in range(5))
            bc = lambda v: v.unsqueeze(2).to_broadcast([P, 2 * T, C])
            sq = H0A[:, :, 0:C] if tag == 0 else H1[:, :, :, :].rearrange("p t b c -> p (t b) c")
            a = DV.do(lambda e: e.tensor_reduce(sums, src, AX, ALU.add), *waits)
            a = DV.do(lambda e: e.tensor_scalar(mean, sums, 1.0 / C, None, ALU.mult), a)
            a = DV.do(lambda e: e.tensor_tensor(XC[:, :, :], src, bc(mean), ALU.subtract), a)
            a = DV.do(lambda e: e.tensor_tensor(sq, XC[:, :, :], XC[:, :, :], ALU.mult), a)
            a = DV.do(lambda e: e.tensor_reduce(var, sq, AX, ALU.add), a)
            a = AC.do(lambda e: e.activation(sd, var, ACT.Sqrt, bias=CF[:, CF_EPS:CF_EPS + 1],
                                             scale=1.0 / C), a, c_all)
            a = DV.do(lambda e: e.reciprocal(rs, sd), a)
            for i, o in enumerate(outs):
                r = ST[:, 4, T * i:T * i + T].unsqueeze(2).to_broadcast([P, T, C])
                xc = XC[:, T * i:T * i + T, :]
                last = DV.do(lambda e, o=o, r=r, xc=xc: e.scalar_tensor_tensor(
                    out=o, in0=xc, scalar=0.0, in1=r, op0=ALU.max, op1=ALU.mult), a)
            return last

        def load_x(g):
            sl = g % 2
            t = None
            for i in range(2):
                t = dma(X[:, sl, i], x_d[2 * g + i].rearrange("(t p) c -> p t c", p=P), s_x[sl],
                        32 * (g // 2) + 16 * (i + 1), x_free[sl])
            x_ready[g] = t

        def prepare(g):
            nonlocal adj_n
            sl = g % 2
            if g == 0:
                load_x(0)
            xs = X[:, sl].rearrange("p b t c -> p (b t) c")
            t_h0 = layernorm_relu(xs, [H0A[:, T * i:T * i + T, 0:C] for i in range(2)],
                                  [x_ready[g], t_one, tok.get("h0_read"), tok.get("xc_read")], 0)
            yield
            for b in range(2):
                t_cum = []
                t_nei = []
                for t in range(T):
                    bt = 2 * g + b
                    k = adj_n % NADJ
                    adj_n += 1
                    got = dma(ADJ[:, k, :], adj_d[bt, t * P:t * P + P, :], s_adj[k],
                              16 * ((adj_n - 1) // NADJ + 1), *(adj_free[k] or ()))
                    a = ADJ[:, k, :]
                    nei = NEI[:, t * N:t * N + N]
                    nd0 = nei[:, t * P:t * P + P]
                    d = DV.do(lambda e, nei=nei, a=a: e.tensor_scalar(nei, a, 0.0, None, ALU.is_gt),
                              got, tok.get("oh_read") if b == 0 else tok.get("nei_read"))
                    d2 = DV.do(lambda e, nd0=nd0: e.tensor_tensor(nd0, nd0, CH[:, CH_OFF, :], ALU.mult),
                               d, c_all)
                    t_nei.append(d2)
                    d3 = DV.do(lambda e, t=t, nei=nei: e.tensor_tensor_scan(
                        CUM[:, t * N:t * N + N], nei, nei, 0.0, ALU.add, ALU.max), d2,
                        tok.get("oh_read") if b == 0 else tok.get("nei_read"))
                    t_cum.append(d3)
                    for hf in range(2):
                        bk = ring("T")
                        for j in range(4):
                            c0 = (4 * hf + j) * P
                            tp = PE.do(lambda e, bk=bk, j=j, a=a, c0=c0: e.transpose(
                                banks[bk][:, j * P:j * P + P], a[:, c0:c0 + P], idf),
                                got, c_all, free[bk] if j == 0 else None)
                        i2 = st["AT"] % 2
                        st["AT"] += 1
                        ev = AC.do(lambda e, bk=bk, i2=i2: e.activation(
                            ADJT[:, i2], banks[bk][:, :].rearrange("p (k n) -> p k n", n=P), ACT.Copy),
                            tp, at_free[i2])
                        free[bk] = ev
                        for j in range(4):
                            kt = 4 * hf + j
                            mm = PE.do(lambda e, i2=i2, j=j, kt=kt, b=b, t=t: e.matmul(
                                banks["L"][:, 65 * (t % 4):65 * (t % 4) + 65], ADJT[:, i2, j, :],
                                H0A[:, T * b + kt, :], start=(kt == 0), stop=(kt == T - 1),
                                skip_group_check=True),
                                ev if j == 0 else None, t_h0, free["L"] if t % 4 == 0 else None)
                        at_free[i2] = mm
                    adj_free[k] = (tp, d)
                    if t % 4 == 3:
                        t0 = t - 3
                        lv = banks["L"][:, 0:260].rearrange("p (t c) -> p t c", c=65)
                        dg = ST[:, 5, 4 * (t0 // 4):4 * (t0 // 4) + 4]
                        q = DV.do(lambda e, dg=dg, lv=lv: e.tensor_scalar(
                            dg, lv[:, :, 64], 1.0, None, ALU.max), mm, tok.get("dg_read"))
                        q = DV.do(lambda e, dg=dg: e.reciprocal(dg, dg), q)
                        msg = XC[:, T * b + t0:T * b + t0 + 4, :]
                        q = DV.do(lambda e, dg=dg, lv=lv, msg=msg: e.tensor_tensor(
                            msg, lv[:, :, 0:64], dg.unsqueeze(2).to_broadcast([P, 4, C]), ALU.mult),
                            q, t_h0)
                        free["L"] = q
                        tok["dg_read"] = q
                        xv = X[:, sl, b, t0:t0 + 4, :]
                        t_x1 = DV.do(lambda e, xv=xv, msg=msg: e.tensor_tensor(xv, xv, msg, ALU.add), q)
                    if b == 1 and t == T - 1:
                        tok["h0_read"] = mm
                    yield
                nb, u, sk, a15, hh, v = (SK[:, i, :] for i in range(6))
                cumv = CUM.rearrange("p (t n) -> p t n", n=N)
                mk = MK[:, (2 * g + b) * T:(2 * g + b) * T + T]
                q = PO.do(lambda e, cumv=cumv, nb=nb: e.tensor_copy(nb, cumv[:, :, N - 1]), t_cum[-1],
                          tok.get("sk_read"))
                q1 = PO.do(lambda e, nb=nb, u=u: e.tensor_scalar(u, nb, 10.0, None, ALU.is_gt), q)
                q1 = PO.do(lambda e, u=u, mk=mk: e.tensor_tensor(u, u, mk, ALU.mult), q1, t_mk)
                q = PO.do(lambda e, nb=nb, sk=sk: e.tensor_scalar(sk, nb, 0.5, 0.25, ALU.mult, ALU.add), q)
                q = PO.do(lambda e, sk=sk: e.tensor_scalar(sk, sk, 8388608.0, None, ALU.add), q)
                q = PO.do(lambda e, sk=sk: e.tensor_scalar(sk, sk, -8388608.0, None, ALU.add), q)
                q2 = PO.do(lambda e, sk=sk, v=v: e.tensor_scalar(v, sk, -1.5, None, ALU.mult), q)
                q2 = PO.do(lambda e, v=v, u=u, a15=a15: e.tensor_tensor(a15, v, u, ALU.mult), q2)
                q3 = PO.do(lambda e, sk=sk, hh=hh: e.tensor_scalar(hh, sk, 0.5, -NOMATCH, ALU.mult, ALU.add), q2)
                q3 = PO.do(lambda e, u=u, hh=hh: e.tensor_tensor(hh, hh, u, ALU.mult), q3)
                q3 = PO.do(lambda e, hh=hh: e.tensor_scalar(hh, hh, NOMATCH, None, ALU.add), q3)
                t_rem = []
                for t in range(T):
                    cu, ne = CUM[:, t * N:t * N + N], NEI[:, t * N:t * N + N]
                    w = PO.do(lambda e, cu=cu, ne=ne: e.tensor_tensor(cu, cu, ne, ALU.mult), q3,
                              t_cum[t])
                    w = AC.do(lambda e, cu=cu, t=t: e.activation(cu, cu, ACT.Abs, bias=SK[:, 3, t:t + 1]),
                              w)
                    t_rem.append(w)
                yield
                for t in range(T):
                    cu = CUM[:, t * N:t * N + N]
                    w = DV.do(lambda e, cu=cu, t=t: e.tensor_scalar(cu, cu, SK[:, 4, t:t + 1], None,
                                                                    ALU.is_equal), t_rem[t])
                tok["sk_read"] = w
                t_rem = w
                yield
                nd = POS[:, b]
                for k in range(T):
                    for ch in range(2):
                        bk = ring("S")

                        def score(e, bk=bk, k=k, ch=ch):
                            o = banks[bk]
                            for j in range(4):
                                t = 4 * ch + j
                                oj = o[:, j * P:j * P + P]
                                at = t * N + k * P
                                e.matmul(oj, NEI[:, at:at + P], CH[:, CH_ID, :], start=(j == 0),
                                         stop=False, skip_group_check=True)
                                e.matmul(oj, CUM[:, at:at + P], CH[:, CH_NEG, :], start=False,
                                         stop=False, skip_group_check=True)
                                if t == k:
                                    e.matmul(oj, CH[:, CH_ID, :], CH[:, CH_ID, :], start=False,
                                             stop=False, skip_group_check=True)
                            return e.matmul(o[:, :], CH[:, CH_NEG, :],
                                            CUM[:, k * N + 512 * ch:k * N + 512 * ch + 512],
                                            start=False, stop=True, skip_group_check=True)
                        w = PE.do(score, t_rem, t_nei[-1], free[bk])
                        ndc = nd[:, k, 512 * ch:512 * ch + 512]
                        free[bk] = AC.do(lambda e, ndc=ndc, bk=bk: e.activation(ndc, banks[bk][:, :],
                                                                              ACT.Relu), w,
                                         tok.get("pos_read"))
                    if k % 4 == 3:
                        yield
                tok["nei_read"] = w
                t_nd = free[bk]
                for ch in range(2):
                    bk = ring("S")
                    cs = slice(512 * ch, 512 * ch + 512)

                    def total(e, bk=bk, cs=cs, nd=nd):
                        for k in range(T):
                            m = e.matmul(banks[bk][:, :], CH[:, CH_ONE, :], nd[:, k, cs],
                                         start=(k == 0), stop=(k == T - 1))
                        return m
                    w = PE.do(total, t_nd, free[bk])
                    hs = slice(C * b, C * b + C)
                    AC.do(lambda e, bk=bk, cs=cs, hs=hs: e.activation(
                        NVN[hs, cs], banks[bk][hs, :], ACT.Copy, scale=-PAD), w, tok.get("nvn_read"))
                    for i, (n0, n1, d) in enumerate(CLASSES):
                        lo, hi = max(n0, 512 * ch), min(n1, 512 * ch + 512)
                        if lo < hi:
                            AC.do(lambda e, bk=bk, lo=lo, hi=hi, i=i, ch=ch, b=b: e.activation(
                                FL[0:1, b, lo:hi], banks[bk][0:1, lo - 512 * ch:hi - 512 * ch], ACT.Relu,
                                bias=CF[0:1, CF_CAP + i:CF_CAP + i + 1]), w, tok.get("fl_read"))
                    for q in range(3):
                        r = AC.do(lambda e, bk=bk, q=q: e.activation(
                            RQ[:, q, :], banks[bk][:, :], ACT.Abs, scale=TAUS[q],
                            bias=CF[:, CF_BIASQ + q:CF_BIASQ + q + 1]), w, tok.get("rq_read"))
                    free[bk] = r
                    for q in range(3):
                        r = AC.do(lambda e, q=q: e.activation(
                            RQ[:, q, :], RQ[:, q, :], ACT.Relu, scale=-WTS[q],
                            bias=CF[:, CF_WQ + q:CF_WQ + q + 1]), free[bk])
                    co = COEF[:, b, cs]
                    r = PO.do(lambda e, co=co: e.tensor_tensor(co, RQ[:, 0, :], RQ[:, 1, :], ALU.add), r,
                              tok.get("coef_read"))
                    r = PO.do(lambda e, co=co: e.tensor_tensor(co, co, RQ[:, 2, :], ALU.add), r)
                    tok["rq_read"] = r
                    tok["coef", b] = r
                yield
                for k in reversed(range(T)):
                    for ch in range(2):
                        bk = ring("S")
                        cs = slice(512 * ch, 512 * ch + 512)

                        def place(e, bk=bk, k=k, cs=cs, nd=nd):
                            for j in range(k + 1):
                                m = e.matmul(banks[bk][:, :], CH[:, CH_PRE if j == k else CH_ONE, :],
                                             nd[:, j, cs], start=(j == 0), stop=(j == k))
                            return m
                        w = PE.do(place, t_nd, free[bk])
                        free[bk] = AC.do(lambda e, k=k, cs=cs, bk=bk, nd=nd: e.activation(
                            nd[:, k, cs], banks[bk][:, :], ACT.Copy), w)
                    if k % 4 == 0:
                        yield
                tok["pos", b] = free[bk]
            w = PO.do(lambda e: e.tensor_tensor(FL[:, 0, :], FL[:, 0, :], FL[:, 1, :], ALU.add),
                      tok["pos", 1])
            tok["any"] = DV.do(lambda e, g=g: e.tensor_reduce(ANY[0:1, g:g + 1], FL[:, 0, :], AX, ALU.add),
                               w)
            xs = X[:, sl].rearrange("p b t c -> p (b t) c")
            t_h1 = layernorm_relu(xs, [H1[:, :, i, :] for i in range(2)], [t_x1, tok.get("h1_read")], 1)
            tok["xc_read"] = t_h1
            yield
            for i in range(2):
                h1, hi, lo = H1[:, :, i, :], HL[:, 0, i], HL[:, 1, i]
                w = AC.do(lambda e, h1=h1, hi=hi: e.activation(hi, h1, ACT.Copy, scale=HSCALE), t_h1,
                          tok.get("oh_read"))
                w = DV.do(lambda e, h1=h1, hi=hi, lo=lo: e.scalar_tensor_tensor(
                    out=lo, in0=h1, scalar=HSCALE, in1=hi, op0=ALU.mult, op1=ALU.subtract), w)
            tok["hl"] = w
            for hf in range(2):
                bk = ring("T")
                for j in range(4):
                    h1 = H1[:, 4 * hf + j].rearrange("p b c -> p (b c)")
                    tp = PE.do(lambda e, bk=bk, j=j, h1=h1: e.transpose(
                        banks[bk][:, j * P:j * P + P], h1, idf), t_h1, free[bk] if j == 0 else None)
                free[bk] = AC.do(lambda e, bk=bk, hf=hf: e.activation(
                    H1T[:, 512 * hf:512 * hf + 512], banks[bk][:, :], ACT.Copy), tp, tok.get("h1t_read"))
            tok["h1_read"] = tp
            tok["h1t"] = free[bk]
            if g + 1 < NP:
                load_x(g + 1)
            yield

        def overflow(g, my):
            g0, g1 = banks["G0"], banks["G1"]
            any_ap = ANY[0:1, g:g + 1].bitcast(I32)
            fl_ap = FL[0:1, 0, :].bitcast(I32)
            va, vb = SL[:, 0:2, :].rearrange("p a n -> p (a n)")[:, 0:N], \
                SL[:, 2:4, :].rearrange("p a n -> p (a n)")[:, 0:N]
            wt = SL[:, 4:6, :].rearrange("p a n -> p (a n)")[:, 0:N]
            io = SL[:, 6:8, :].rearrange("p a n -> p (a n)")[:, 0:N]
            u = SL[:, 8:10, :].rearrange("p a n -> p (a n)")[:, 0:N]
            u2 = SL[:, 10:12, :].rearrange("p a n -> p (a n)")[:, 0:N]

            def on_pe(e):
                flag = e.value_load(any_ap)
                with e.If(flag):
                    with e.Fori(0, N // 2) as i:
                        f = e.value_load(fl_ap[:, bass.ds(i, 1)])
                        with e.If(f):
                            for _ in range(2):
                                e.wait_ge(f_d, 1)
                                e.sem_clear(f_d)
                                for k in range(T):
                                    gb = (g0, g1)[k // 4]
                                    for b in range(2):
                                        mm = e.matmul(gb[C * b:C * b + C, (k % 4) * P:(k % 4) * P + P],
                                                      COL[:, b, k, :].to_broadcast([P, C]),
                                                      CH[:, CH_ID, :], start=(k % 4 == 0),
                                                      stop=(k % 4 == 3), skip_group_check=True)
                                mm.then_inc(f_p, 1)
                return e.nop()

            def on_dve(e):
                def link(ins):
                    ins.then_inc(f_l, 1)
                    e.wait_ge(f_l, 1)
                    e.sem_clear(f_l)

                flag = e.value_load(any_ap)
                with e.If(flag):
                    link(e.memset(u, 1.0))
                    link(e.tensor_tensor_scan(io, u, u, 0.0, ALU.add, ALU.max))
                    with e.Fori(0, N // 2) as i:
                        f = e.value_load(fl_ap[:, bass.ds(i, 1)])
                        with e.If(f):
                            for odd in range(2):
                                for b in range(2):
                                    link(e.tensor_copy(COL[:, b], POS[:, b, :, bass.ds(i * 2 + odd, 1)]))
                                e.sem_inc(f_d, 1)
                                e.wait_ge(f_p, 1)
                                e.sem_clear(f_p)
                                for j, gb in enumerate((g0, g1)):
                                    link(e.tensor_scalar(va[:, 512 * j:512 * j + 512], gb[:, :], 1024.5,
                                                         BIG, ALU.is_lt, ALU.mult))
                                link(e.tensor_tensor(va, va, H1T[:, :], ALU.max))
                                cur, nxt = va, vb
                                for p, k in merge_stages(N):
                                    c3 = cur.rearrange("q (n o) -> q n o", o=1)
                                    n3 = nxt.rearrange("q (n o) -> q n o", o=1)
                                    a0, a1, ar = stage_views(c3, p, k)
                                    b0, b1, br = stage_views(n3, p, k)
                                    link(e.tensor_tensor(b0, a0, a1, ALU.min))
                                    link(e.tensor_tensor(b1, a0, a1, ALU.max))
                                    if ar is not None:
                                        link(e.tensor_copy(br, ar))
                                    cur, nxt = nxt, cur
                                nv = FB[:, 0:1]
                                link(e.tensor_copy(nv, NVN[:, bass.ds(i * 2 + odd, 1)]))
                                link(e.memset(wt, 0.0))
                                for q in range(3):
                                    link(e.tensor_scalar(FB[:, 1:2], nv, -TAUS[q] / PAD, 1.0 - TAUS[q],
                                                         ALU.mult, ALU.add))
                                    link(e.tensor_scalar(u, io, FB[:, 1:2], None, ALU.subtract))
                                    link(e.tensor_scalar(u2, u, -1.0, None, ALU.mult))
                                    link(e.tensor_tensor(u, u, u2, ALU.min))
                                    link(e.tensor_scalar(u, u, 1.0, 0.0, ALU.add, ALU.max))
                                    link(e.scalar_tensor_tensor(out=wt, in0=u, scalar=WTS[q], in1=wt,
                                                                op0=ALU.mult, op1=ALU.add))
                                link(e.tensor_tensor(nxt, cur, wt, ALU.mult))
                                link(e.tensor_reduce(FB[:, 2:3], nxt, AX, ALU.add))
                                link(e.tensor_tensor(ZF[:, bass.ds(i * 2 + odd, 1)], FB[:, 2:3],
                                                     H1T[:, bass.ds(i * 2 + odd, 1)], ALU.add))
                return e.nop()

            my["any_pe"] = PE.do(on_pe, tok["any"], tok["pos", 0], tok["pos", 1], free["G0"], free["G1"],
                                 c_all)
            my["zf"] = DV.do(on_dve, tok["any"], tok["h1t"], t_zf, my["any_pe_wait"], tok.get("sl_read"),
                             *tok.get("last_dve", ()))

        def chunks_of(ci):
            n0, n1, d = CLASSES[ci]
            w = n1 - n0
            if ci == 3:
                return [(0, 512, j, 1) for j in range(d)] + [(512, 256, j, 2) for j in range(0, d, 2)]
            per = 512 // w
            return [(0, w, j, min(per, d - j)) for j in range(0, d, per)]

        class Chunk:
            pass

        def gather(ci, lane0, w, d0, nd, my):
            n0 = CLASSES[ci][0] + lane0
            c = Chunk()
            c.cols = w * nd
            r = st["OH"] = (st.get("OH", -1) + 1) % 2
            c.bk = ring("G")
            bk = c.bk
            take_up(bk)
            ohs = []
            for b in range(2):
                oh = OHB[:, (2 * r + b) * 4096:(2 * r + b) * 4096 + T * c.cols]\
                    .rearrange("p (k c) -> p k c", k=T)
                ps = POS[:, b, :, n0:n0 + w]
                waits = (tok["pos", b], oh_free[r], tok["nei_read"])
                if ci == 0:
                    for k4 in range(2):
                        ov = oh[:, 4 * k4:4 * k4 + 4, :].rearrange("p k (d n) -> p k d n", n=w)
                        pv = ps[:, 4 * k4:4 * k4 + 4, :].unsqueeze(2).to_broadcast([P, 4, nd, w])
                        iv = CH[:, CH_IOTA, d0:d0 + nd].unsqueeze(1).unsqueeze(3)\
                            .to_broadcast([P, 4, nd, w])
                        for kk in range(4):
                            t = DV.do(lambda e, ov=ov, pv=pv, iv=iv, kk=kk: e.tensor_tensor(
                                ov[:, kk], pv[:, kk], iv[:, kk], ALU.is_equal), *waits, c_all)
                else:
                    for j in range(nd):
                        t = DV.do(lambda e, oh=oh, ps=ps, j=j, d=d0 + j, w=w: e.tensor_scalar(
                            oh[:, :, j * w:j * w + w], ps, float(N + 1 + d), None, ALU.is_equal), *waits)
                ohs.append(oh)
            def mms(e):
                for k in range(T):
                    for part in range(2):
                        for b in range(2):
                            m = e.matmul(banks[bk][C * b:C * b + C, 0:c.cols], HL[:, part, b, k, :],
                                         ohs[b][:, k, :], start=(k == 0 and part == 0),
                                         stop=(k == T - 1 and part == 1), skip_group_check=True)
                return m
            c.mm = PE.do(mms, t, tok["hl"], free[bk])
            oh_free[r] = c.mm
            tok["oh_last"] = c.mm
            c.args = (ci, lane0, w, d0, nd)
            return c

        def evacuate(c, slot, *waits):
            ci, lane0, w, d0, nd = c.args
            n0 = CLASSES[ci][0] + lane0
            for j in range(nd):
                t = DV.do(lambda e, j=j, w=w, n0=n0, d=d0 + j, bk=c.bk: e.scalar_tensor_tensor(
                    out=slot(d)[:, lane0:lane0 + w], in0=NVN[:, n0:n0 + w], scalar=PAD * (d + 1),
                    in1=banks[bk][:, j * w:j * w + w], op0=ALU.add, op1=ALU.max), c.mm, *waits)
            free[c.bk] = t
            return t

        def take_up(bk):
            if bk in pending:
                pending.pop(bk)()

        def gather_all(ci, slot, my, *waits):
            for a in chunks_of(ci):
                c = gather(ci, *a, my)

                def up(c=c):
                    my["ev", ci] = evacuate(c, slot, *waits)
                take_up("G1" if c.bk == "G0" else "G0")
                pending[c.bk] = up
                yield
            take_up(c.bk)

        def batcher(ci, my):
            n0, n1, d = CLASSES[ci]
            w = n1 - n0
            cur, nxt = (v[:, 0:d * w].rearrange("p (d n) -> p d n", n=w) for v in (SA, SB))
            t = my["ev", ci]
            for p, k in merge_stages(d):
                a0, a1, ar = stage_views(cur, p, k)
                b0, b1, br = stage_views(nxt, p, k)
                wb = (t, tok.get("sb_read"))
                t = DV.do(lambda e, b0=b0, a0=a0, a1=a1: e.tensor_tensor(b0, a0, a1, ALU.min), *wb)
                t = DV.do(lambda e, b1=b1, a0=a0, a1=a1: e.tensor_tensor(b1, a0, a1, ALU.max), *wb)
                if ar is not None:
                    t = DV.do(lambda e, br=br, ar=ar: e.tensor_copy(br, ar), *wb)
                cur, nxt = nxt, cur
                yield
            my["sorted", ci] = (cur, t)

        def coef_rows(ci, lane0, w, d0, nd):
            n0 = CLASSES[ci][0] + lane0
            bk = ring("G")
            take_up(bk)

            def mms(e):
                for b in range(2):
                    o = banks[bk][C * b:C * b + C, 0:w * nd]
                    if ci == 0:
                        ov = o.rearrange("p (d n) -> p d n", n=w)
                        for n in range(w):
                            m = e.matmul(ov[:, :, n], COEF[:, b, n0 + n:n0 + n + 1].to_broadcast([P, C]),
                                         CH[:, CH_SEL, d0:d0 + nd], start=(n == 0), stop=(n == w - 1),
                                         skip_group_check=True)
                    else:
                        for j in range(nd):
                            m = e.matmul(o[:, j * w:j * w + w],
                                         CH[:, CH_SEL, d0 + j:d0 + j + 1].to_broadcast([P, C]),
                                         COEF[:, b, n0:n0 + w], start=(j == 0), stop=(j == nd - 1),
                                         skip_group_check=True)
                return m
            t = PE.do(mms, tok["coef", 0], tok["coef", 1], free[bk], c_all)
            tok["coef_last"] = t
            return bk, t

        def weigh(ci, my):
            n0, n1, d = CLASSES[ci]
            w = n1 - n0
            cur, t = my["sorted", ci]
            flat = cur.rearrange("p d n -> p (d n)")
            for lane0, w_, d0, nd in chunks_of(ci):
                bk, mm = coef_rows(ci, lane0, w_, d0, nd)
                v = flat[:, d0 * w:(d0 + nd) * w]
                t = DV.do(lambda e, v=v, bk=bk, n=nd * w: e.tensor_tensor(v, v, banks[bk][:, 0:n], ALU.mult),
                          t, mm)
                free[bk] = t
                yield
            r = DV.do(lambda e: e.tensor_reduce(RED[:, n0:n1], cur.rearrange("p d n -> p n d"), AX, ALU.add),
                      t, tok.get("red_read"))
            tok["sb_read"] = r
            my["red", ci] = r
            yield

        def network(my):
            loc = list(range(12))
            spare = [(i, None) for i in range(12, NSL)]
            layer = my["ev", 3]
            for level in NET12:
                t = None
                for i, j in level:
                    (la, lb) = loc[i], loc[j]
                    (s1, r1), (s2, r2) = spare.pop(0), spare.pop(0)
                    DV.do(lambda e, la=la, lb=lb, s1=s1: e.tensor_tensor(SL[:, s1, :], SL[:, la, :],
                                                                        SL[:, lb, :], ALU.min), layer, r1)
                    t = DV.do(lambda e, la=la, lb=lb, s2=s2: e.tensor_tensor(SL[:, s2, :], SL[:, la, :],
                                                                            SL[:, lb, :], ALU.max), layer, r2)
                    loc[i], loc[j] = s1, s2
                    spare += [(la, t), (lb, t)]
                    yield
                layer = t
            my["sorted", 3] = (loc, layer)
            my["spare"] = [a for a, _ in spare]

        def weigh_last(my):
            loc, t = my["sorted", 3]
            done = {}
            for lane0, w, d0, nd in chunks_of(3):
                bk, mm = coef_rows(3, lane0, w, d0, nd)
                for j in range(nd):
                    v = SL[:, loc[d0 + j], lane0:lane0 + w]
                    t = DV.do(lambda e, v=v, bk=bk, j=j, w=w: e.tensor_tensor(
                        v, v, banks[bk][:, j * w:j * w + w], ALU.mult), my["sorted", 3][1], mm)
                    d = d0 + j
                    s_ = PE.do(lambda e, v=v, d=d, w=w: e.matmul(
                        banks["M"][:, 0:w], idf, v, start=(d == 0), stop=(d == 11)), t,
                        free["M"] if d == 0 else None)
                free[bk] = t
                yield
                if d0 + nd == 12:
                    z = my["z"]
                    for n in range(256 + lane0, 256 + lane0 + w, 256):
                        zc = z[n // 512][:, n % 512:n % 512 + 256]
                        t = DV.do(lambda e, zc=zc, n=n, lane0=lane0: e.tensor_tensor(
                            zc, banks["M"][:, n - 256 - lane0:n - lane0], H1T[:, n:n + 256], ALU.add), s_)
                    free["M"] = t
                    yield
            my["z1"] = t

        def finish(g, my):
            sl = g % 2
            sp = my["spare"]
            z = my["z"]
            hid = [SL[:, sp[2], 0:512], SB[:, 0:512]]
            tmp = SL[:, sp[3], 0:512]
            t = DV.do(lambda e: e.tensor_tensor(z[0][:, 0:256], RED[:, :], H1T[:, 0:256], ALU.add),
                      my["red", 0], my["red", 1], my["red", 2], my["sorted", 3][1])
            tok["red_read"] = t
            any_ap = ANY[0:1, g:g + 1].bitcast(I32)

            def patch(e):
                def link(ins):
                    ins.then_inc(f_l, 1)
                    e.wait_ge(f_l, 1)
                    e.sem_clear(f_l)

                flag = e.value_load(any_ap)
                with e.If(flag):
                    for ch in range(2):
                        mask = tmp.bitcast(I32)
                        for n0, n1, d in CLASSES:
                            lo, hi = max(n0, 512 * ch), min(n1, 512 * ch + 512)
                            if lo < hi:
                                link(e.tensor_scalar(mask[:, lo - 512 * ch:hi - 512 * ch], NVN[:, lo:hi],
                                                     -PAD * (d + 0.5), None, ALU.is_lt))
                        link(e.copy_predicated(z[ch], mask, ZF[:, 512 * ch:512 * ch + 512]))
                return e.nop()
            t = DV.do(patch, t, my["z1"])
            tok["h1t_read"] = tok["nvn_read"] = tok["fl_read"] = t
            t_z = t
            yield
            hr = [None, None]
            for b in range(2):
                bm = "M"
                for ch in range(2):
                    bk = ring("S")
                    w = PE.do(lambda e, b=b, ch=ch, bk=bk: e.matmul(
                        banks[bk][:, :], W1[C * b:C * b + C, :], z[ch][C * b:C * b + C, :], start=True,
                        stop=True), t_z, free[bk])
                    a = AC.do(lambda e, bk=bk, ch=ch: e.activation(hid[ch], banks[bk][:, :], ACT.Relu,
                                                                  bias=B1[:, 0:1]), w, hr[ch], t_z)
                    free[bk] = a

                    def second(e, ch=ch, bm=bm):
                        for j in range(4):
                            o = banks[bm][:, (4 * ch + j) * C:(4 * ch + j) * C + C]
                            e.matmul(o, hid[ch][:, j * P:j * P + P], W2[:, :], start=(ch == 0 and j == 0),
                                     stop=False, skip_group_check=True)
                            m = e.matmul(o, CF[0:1, CF_ONE:CF_ONE + P], B2[0:1, :], start=False,
                                         stop=(ch == 1 and j == 3), skip_group_check=True)
                        return m
                    y = PE.do(second, a, free[bm])
                    hr[ch] = y
                mk = MK[:, (2 * g + b) * T:(2 * g + b) * T + T].unsqueeze(2).to_broadcast([P, T, C])
                tv = tmp.rearrange("p (t c) -> p t c", c=C)
                t = DV.do(lambda e, tv=tv, mk=mk, bm=bm: e.tensor_tensor(
                    tv, banks[bm][:, :].rearrange("p (t c) -> p t c", c=C), mk, ALU.mult), y,
                    tok.get("tmp_read"), t_z)
                free[bm] = t
                xv = X[:, sl, b]
                t = PO.do(lambda e, tv=tv, xv=xv: e.tensor_tensor(xv, xv, tv, ALU.add), t)
                tok["tmp_read"] = t
                out_n[sl] += 16
                x_free[sl] = dma(out_d[2 * g + b].rearrange("(t p) c -> p t c", p=P), xv, s_out[sl],
                                 out_n[sl], t)
                yield
            tok["sl_read"] = t
            my["done"] = t
            tok["sb_free"] = y

        def along(main, side):
            main, side = list(main), side
            for _ in main:
                pass

        def run(gen, *others):
            for _ in gen:
                pass

        for _ in prepare(0):
            pass
        for g in range(NP):
            my = {"any_pe_wait": None}
            overflow(g, my)
            slot_a = {}
            for ci in range(3):
                n0, n1, d = CLASSES[ci]
                v = SA[:, 0:d * (n1 - n0)].rearrange("p (d n) -> p d n", n=n1 - n0)
                slot_a[ci] = lambda d_, v=v: v[:, d_, :]
            c3 = gather_all(3, lambda d_: SL[:, d_, :], my, my["zf"], tok.get("sl_read"))

            def some(gen, n):
                for _ in range(n):
                    next(gen, None)

            run(gather_all(0, slot_a[0], my, my["zf"], tok.get("sb_read")))
            some(c3, 4)
            run(batcher(0, my))
            run(weigh(0, my))
            run(gather_all(1, slot_a[1], my, tok.get("sb_read")))
            some(c3, 4)
            run(batcher(1, my))
            run(weigh(1, my))
            run(c3)
            run(gather_all(2, slot_a[2], my, my["red", 0], my["sorted", 1][1]))
            tok["oh_read"] = tok["oh_last"]
            tok["pos_read"] = tok["oh_last"]
            nxt = prepare(g + 1) if g + 1 < NP else iter(())
            keep = dict(tok)

            def tail():
                yield from batcher(2, my)
                yield from weigh(2, my)
                yield from network(my)
                sp = my["spare"]
                my["z"] = [SL[:, sp[0], 0:512], SL[:, sp[1], 0:512]]
                yield from weigh_last(my)
                yield from finish(g, my)
            run(tail())
            tok["coef_read"] = tok["coef_last"]
            run(nxt)

        for lane in (PE, AC, DV, PO, SP):
            lane.count()
        block = ctx.enter_context(nc.Block())

        @block.tensor
        def _(e):
            PE.issue(e)

        @block.scalar
        def _(e):
            AC.issue(e)

        @block.vector
        def _(e):
            DV.issue(e)

        @block.gpsimd
        def _(e):
            PO.issue(e)

        @block.sync
        def _(e):
            SP.issue(e)
            for i in range(2):
                e.wait_ge(s_out[i], out_n[i])


def constants():
    import numpy as np

    cf = np.zeros((P, CF_N), np.float32)
    cf[:, CF_ID:CF_ID + P] = np.eye(P)
    d = np.arange(P)
    for q in range(3):
        cf[:, CF_BIASQ + q] = -(TAUS[q] + d)
        cf[:, CF_WQ + q] = WTS[q]
    cf[:, CF_EPS] = 1e-5
    for i, (_, _, slots) in enumerate(CLASSES):
        cf[:, CF_CAP + i] = -slots
    cf[:, CF_ONE:CF_ONE + P] = 1.0
    ch = np.zeros((P, 7, P), np.float16)
    ch[:, CH_ID] = np.eye(P)
    ch[:, CH_NEG] = -np.eye(P)
    ch[:, CH_PRE] = np.triu(np.ones((P, P))) + N * np.eye(P)
    ch[:, CH_ONE] = 1.0
    ch[:, CH_OFF] = 1.0 - np.eye(P)
    ch[:, CH_IOTA] = N + 1 + d[None, :]
    ch[:, CH_SEL] = np.eye(P) / HSCALE
    return cf, ch


def kernel(x, adj, nodemask, L1_gnn_W1, L1_gnn_b1, L1_gnn_W2, L1_gnn_b2):
    import numpy as np
    import concourse.bacc as bacc
    from concourse.bass_utils import run_bass_kernel_spmd

    nc = bacc.Bacc("TRN2", target_bir_lowering=False, num_devices=1)
    cf, ch = constants()
    given = {
        "x": x, "adj": adj, "nodemask": np.ascontiguousarray(nodemask).view(np.uint8), "w1": L1_gnn_W1,
        "b1": L1_gnn_b1, "w2": L1_gnn_W2, "b2": L1_gnn_b2, "cf": cf, "ch": ch,
    }
    arrays, args = {}, []
    for name, a in given.items():
        a = np.ascontiguousarray(a)
        arrays[f"in_{name}"] = a
        args.append(nc.dram_tensor(f"in_{name}", a.shape, mybir.dt.from_np(a.dtype),
                                   kind="ExternalInput").ap())
    out = nc.dram_tensor("out_0", (B, N, C), F32, kind="ExternalOutput").ap()
    program(nc, *args, out)
    r = run_bass_kernel_spmd(nc, [arrays], core_ids=[0])
    return r.results[0]["out_0"]
```

```python
import itertools
from contextlib import ExitStack

import concourse.bass as bass
from concourse import mybir

ALU = mybir.AluOpType
ACT = mybir.ActivationFunctionType
F32 = mybir.dt.float32
F16 = mybir.dt.float16
I32 = mybir.dt.int32
AX = mybir.AxisListType.X

B, N, C, H = 16, 1024, 64, 128
P = 128
T = N // P
NP = B // 2
TAUS = (0.25, 0.5, 0.75)
WTS = (0.25, 0.5, 0.25)
HSCALE = 4096.0
BIG = 1.0e9
NOMATCH = 9999.0
PREP, LAG, EARLY = 46, 2, 8

CLASSES = [(0, 8, 128), (8, 80, 32), (80, 256, 16), (256, 1024, 11)]
NET11 = [
    [(0, 9), (1, 6), (2, 4), (3, 7), (5, 8)],
    [(0, 1), (3, 5), (4, 10), (6, 9), (7, 8)],
    [(1, 3), (2, 5), (4, 7), (8, 10)],
    [(0, 4), (1, 2), (3, 7), (5, 9), (6, 8)],
    [(0, 1), (2, 6), (4, 5), (7, 8), (9, 10)],
    [(2, 4), (3, 6), (5, 7), (8, 9)],
    [(1, 2), (3, 4), (5, 6), (7, 8)],
    [(2, 3), (4, 5), (6, 7)],
]

CF_ID, CF_BIASQ, CF_WQ, CF_EPS, CF_CAP, CF_ONE, CF_N = 0, 128, 131, 134, 135, 139, 267
(CH_ID, CH_NEG, CH_PRE, CH_ONE, CH_OFF, CH_IOTA, CH_SEL) = range(7)


class Token:

    def __init__(self, lane):
        self.lane, self.used, self.value = lane, False, None


class DmaToken:
    def __init__(self, sem, value):
        self.sem, self.value, self.used = sem, value, True


class Lane:

    def __init__(self, sem):
        self.sem, self.ops = sem, []

    def do(self, fn, *waits):
        t = Token(self)
        for w in waits:
            if w is not None:
                w.used = True
        self.ops.append((fn, [w for w in waits if w is not None], t))
        return t

    def count(self):
        n = 0
        for _, _, t in self.ops:
            if t.used:
                n += 1
                t.value = n

    def issue(self, eng):
        seen = {}
        for fn, waits, t in self.ops:
            for w in waits:
                sem = w.sem if isinstance(w, DmaToken) else w.lane.sem
                if seen.get(id(sem), 0) < w.value:
                    eng.wait_ge(sem, w.value)
                    seen[id(sem)] = w.value
            ins = fn(eng)
            if t.used:
                ins.then_inc(self.sem, 1)


def merge_stages(n):
    p = 1
    while p < n:
        k = p
        while k >= 1:
            yield p, k
            k //= 2
        p *= 2


def stage_views(x, p, k):
    if k == p:
        v = x.rearrange("q (b h p) n -> q b h (p n)", h=2, p=p)
        return v[:, :, 0, :], v[:, :, 1, :], None
    c = 2 * p // k
    v = x.rearrange("q (b c k) n -> q b c (k n)", c=c, k=k)
    return v[:, :, 1:c - 1:2, :], v[:, :, 2:c:2, :], v[:, :, 0:c:c - 1, :]


def program(nc, x_d, adj_d, mask_d, w1_d, b1_d, w2_d, b2_d, cf_d, ch_d, out_d):
    with ExitStack() as ctx:
        def sb(name, shape, dt=F32):
            return ctx.enter_context(nc.sbuf_tensor(name, shape, dt))

        def sem(name):
            return ctx.enter_context(nc.semaphore(name))

        banks = {k: ctx.enter_context(nc.psum_tensor("ps" + k, [P, 512], F32))
                 for k in ("T0", "T1", "L", "S0", "S1", "G0", "G1", "M")}

        X = sb("X", [P, 2, 2, T, C])
        H0A = sb("H0A", [P, 2 * T, C + 1])
        XC = sb("XC", [P, 2 * T, C])
        H1 = sb("H1", [P, T, 2, C])
        HL = sb("HL", [P, 2, 2, T, C], F16)
        NADJ = 4
        ADJ = sb("ADJ", [P, NADJ, N])
        ADJT = sb("ADJT", [P, 2, 4, P])
        OHB = sb("OHB", [P, 16384], F16)
        NEI = OHB[:, 0:8192]
        CUM = OHB[:, 8192:16384]
        POS = sb("POS", [P, 2, T, N], F16)
        NSL = 15
        SL = sb("SL", [P, NSL, 768])
        SA = sb("SA", [P, 16 * 176])
        SB = sb("SB", [P, 16 * 176])
        RED = sb("RED", [P, 256])
        SZ = sb("SZ", [P, 1024])
        COEF = sb("COEF", [P, 2, 2, N], F16)
        RQ = sb("RQ", [P, 3, 512], F16)
        H1T = sb("H1T", [P, N])
        ZF = sb("ZF", [P, N])
        FL = sb("FL", [1, N], F16)
        FLO = sb("FLO", [1, 512], F16)
        ANY = sb("ANY", [1, NP])
        CF = sb("CF", [P, CF_N])
        CH = sb("CH", [P, 7, P], F16)
        W1 = sb("W1", [P, H])
        W2 = sb("W2", [P, C])
        B1 = sb("B1", [P, 1])
        B2 = sb("B2", [1, C])
        MU8 = sb("MU8", [P, P], mybir.dt.uint8)
        MKF = SL[:, 0, 0:128]
        MK = sb("MK", [P, B * T])
        ST = sb("ST", [P, 6, 2 * T])
        SK = sb("SK", [P, 8, T])
        FB = sb("FB", [P, 4])
        MARK = sb("MARK", [P, 1])
        COL = sb("COL", [P, 2, T, 1], F16)

        s = {k: sem("s_" + k) for k in ("pe", "act", "dve", "pool", "sp")}
        PE, AC, DV, PO, SP = (Lane(s[k]) for k in ("pe", "act", "dve", "pool", "sp"))
        s_adj = [sem(f"s_adj{i}") for i in range(NADJ)]
        s_x = [sem(f"s_x{i}") for i in range(2)]
        s_out = [sem(f"s_out{i}") for i in range(2)]
        s_c = sem("s_c")
        f_p, f_d, f_l, f_e = sem("f_p"), sem("f_d"), sem("f_l"), sem("f_e")

        idf = CF[:, CF_ID:CF_ID + P]

        def dma(dst, src, sm, value, *waits):
            SP.do(lambda e: Done(e.dma_start(dst, src).then_inc(sm, 16)), *waits)
            return DmaToken(sm, value)

        class Done:

            def __init__(self, ins):
                self.ins = ins

        n_c = 0

        def const(dst, src):
            nonlocal n_c
            n_c += 16
            return dma(dst, src, s_c, n_c)

        const(CF[:, :], cf_d)
        const(CH[:, :, :], ch_d)
        const(W1[0:C, :], w1_d)
        const(W1[C:P, :], w1_d)
        const(W2[:, :], w2_d)
        const(B1[:, :], b1_d.rearrange("(h o) -> h o", o=1))
        const(B2[:, :], b2_d.rearrange("(o c) -> o c", o=1))
        c_all = const(MU8[:, :], mask_d.rearrange("b (t p) -> (b t) p", p=P))
        t_one = DV.do(lambda e: e.memset(H0A[:, :, C:C + 1], 1.0))
        t = DV.do(lambda e: e.tensor_copy(MKF, MU8[:, :]), c_all)
        t = PE.do(lambda e: e.transpose(banks["M"][:, 0:P], MKF, idf), t, c_all)
        t_mk = DV.do(lambda e: e.tensor_copy(MK[:, :], banks["M"][:, 0:P]), t)
        free = {k: None for k in banks}
        free["M"] = t_mk

        adj_n, adj_free = 0, [None] * NADJ
        at_free = [None, None]
        st = {"T": 0, "S": 0, "G": 0, "AT": 0}

        def ring(kind):
            k = f"{kind}{st[kind] % 2}"
            st[kind] += 1
            return k

        tok = {}
        oh_free = [None, None]
        x_ready, x_free = {}, {0: None, 1: None}
        out_n = [0, 0]

        def layernorm_relu(src, outs, waits, tag):
            sums, mean, var, sd, rs = (ST[:, i, :] for i in range(5))
            bc = lambda v: v.unsqueeze(2).to_broadcast([P, 2 * T, C])
            sq = H0A[:, :, 0:C] if tag == 0 else H1[:, :, :, :].rearrange("p t b c -> p (t b) c")
            a = DV.do(lambda e: e.tensor_reduce(sums, src, AX, ALU.add), *waits)
            a = DV.do(lambda e: e.tensor_scalar(mean, sums, 1.0 / C, None, ALU.mult), a)
            a = DV.do(lambda e: e.tensor_tensor(XC[:, :, :], src, bc(mean), ALU.subtract), a)
            a = DV.do(lambda e: e.tensor_tensor(sq, XC[:, :, :], XC[:, :, :], ALU.mult), a)
            a = DV.do(lambda e: e.tensor_reduce(var, sq, AX, ALU.add), a)
            a = AC.do(lambda e: e.activation(sd, var, ACT.Sqrt, bias=CF[:, CF_EPS:CF_EPS + 1],
                                             scale=1.0 / C), a, c_all)
            a = DV.do(lambda e: e.reciprocal(rs, sd), a)
            for i, o in enumerate(outs):
                r = ST[:, 4, T * i:T * i + T].unsqueeze(2).to_broadcast([P, T, C])
                xc = XC[:, T * i:T * i + T, :]
                last = DV.do(lambda e, o=o, r=r, xc=xc: e.scalar_tensor_tensor(
                    out=o, in0=xc, scalar=0.0, in1=r, op0=ALU.max, op1=ALU.mult), a)
            return last

        def load_x(g):
            sl = g % 2
            t = None
            for i in range(2):
                t = dma(X[:, sl, i], x_d[2 * g + i].rearrange("(t p) c -> p t c", p=P), s_x[sl],
                        32 * (g // 2) + 16 * (i + 1), x_free[sl])
            x_ready[g] = t

        def first_norm(g):
            xs = X[:, g % 2].rearrange("p b t c -> p (b t) c")
            tok["h0"] = layernorm_relu(xs, [H0A[:, T * i:T * i + T, 0:C] for i in range(2)],
                                       [x_ready[g], t_one, tok.get("h0_read"), tok.get("xc_read")], 0)

        def second_norm(g):
            xs = X[:, g % 2].rearrange("p b t c -> p (b t) c")
            t_h1 = layernorm_relu(xs, [H1[:, :, i, :] for i in range(2)],
                                  [tok["x1"], tok.get("h1_read")], 1)
            tok["xc_read"] = t_h1
            for i in range(2):
                h1, hi, lo = H1[:, :, i, :], HL[:, 0, i], HL[:, 1, i]
                w = AC.do(lambda e, h1=h1, hi=hi: e.activation(hi, h1, ACT.Copy, scale=HSCALE), t_h1,
                          tok.get("oh_read"))
                w = DV.do(lambda e, h1=h1, hi=hi, lo=lo: e.scalar_tensor_tensor(
                    out=lo, in0=h1, scalar=HSCALE, in1=hi, op0=ALU.mult, op1=ALU.subtract), w)
            tok["hl"] = w
            tok["h1"] = t_h1

        def first_layer(g, b, t_cum, t_nei):
            nonlocal adj_n
            sl = g % 2
            late = []

            def messages(t, hf, i2, ev):
                for j in range(4):
                    kt = 4 * hf + j
                    mm = PE.do(lambda e, j=j, kt=kt: e.matmul(
                        banks["L"][:, 65 * (t % 4):65 * (t % 4) + 65], ADJT[:, i2, j, :],
                        H0A[:, T * b + kt, :], start=(kt == 0), stop=(kt == T - 1),
                        skip_group_check=True),
                        ev if j == 0 else None, tok["h0"], free["L"] if t % 4 == 0 else None)
                at_free[i2] = mm
                if b == 1 and t == T - 1:
                    tok["h0_read"] = mm
                if t % 4 == 3 and hf == 1:
                    t0 = t - 3
                    lv = banks["L"][:, 0:260].rearrange("p (t c) -> p t c", c=65)
                    dg = ST[:, 5, 4 * (t0 // 4):4 * (t0 // 4) + 4]
                    q = DV.do(lambda e: e.tensor_scalar(dg, lv[:, :, 64], 1.0, None, ALU.max), mm,
                              tok.get("dg_read"))
                    q = DV.do(lambda e: e.reciprocal(dg, dg), q)
                    msg = XC[:, T * b + t0:T * b + t0 + 4, :]
                    q = DV.do(lambda e: e.tensor_tensor(
                        msg, lv[:, :, 0:64], dg.unsqueeze(2).to_broadcast([P, 4, C]), ALU.mult),
                        q, tok["h0"])
                    free["L"] = tok["dg_read"] = q
                    xv = X[:, sl, b, t0:t0 + 4, :]
                    tok["x1"] = PO.do(lambda e: e.tensor_tensor(xv, xv, msg, ALU.add), q)

            for t in range(T):
                k = adj_n % NADJ
                adj_n += 1
                a = ADJ[:, k, :]
                got = dma(a, adj_d[2 * g + b, t * P:t * P + P, :], s_adj[k],
                          16 * ((adj_n - 1) // NADJ + 1), *(adj_free[k] or ()))
                nei = NEI[:, t * N:t * N + N]
                nd0 = nei[:, t * P:t * P + P]
                before = tok.get("nei_read")
                d = AC.do(lambda e, nei=nei, a=a: e.activation(nei, a, ACT.Sign), got, before)
                d2 = AC.do(lambda e, nei=nei: e.activation(nei, nei, ACT.Relu), d)
                d2 = PO.do(lambda e, nd0=nd0: e.tensor_tensor(nd0, nd0, CH[:, CH_OFF, :], ALU.mult),
                           d2, c_all)
                t_nei.append(d2)
                cu = CUM[:, t * N:t * N + N]
                d3 = DV.do(lambda e, cu=cu, nei=nei: e.tensor_tensor_scan(
                    cu, nei, nei, 0.0, ALU.add, ALU.max), d2, before)
                d3 = PO.do(lambda e, cu=cu, t=t: e.tensor_copy(SK[:, 0, t:t + 1], cu[:, N - 1:N]), d3,
                           tok.get("sk_read"))
                t_cum.append(PO.do(lambda e, cu=cu, nei=nei: e.tensor_tensor(cu, cu, nei, ALU.mult), d3))
                for hf in range(2):
                    bk = ring("T")
                    for j in range(4):
                        c0 = (4 * hf + j) * P
                        tp = PE.do(lambda e, bk=bk, j=j, a=a, c0=c0: e.transpose(
                            banks[bk][:, j * P:j * P + P], a[:, c0:c0 + P], idf),
                            got, c_all, free[bk] if j == 0 else None)
                    if late:
                        messages(*late.pop())
                    i2 = st["AT"] % 2
                    st["AT"] += 1
                    ev = AC.do(lambda e, bk=bk, i2=i2: e.activation(
                        ADJT[:, i2], banks[bk][:, :].rearrange("p (k n) -> p k n", n=P), ACT.Copy),
                        tp, at_free[i2])
                    free[bk] = ev
                    late.append((t, hf, i2, ev))
                adj_free[k] = (tp, d)
                yield
            messages(*late.pop())

        def thin(g, b, t_cum, t_nei):
            nb, u, sk, a15, hh, v = (SK[:, i, :] for i in range(6))
            mk = MK[:, (2 * g + b) * T:(2 * g + b) * T + T]
            ps = PO.do
            q = ps(lambda e: e.tensor_scalar(u, nb, 10.0, None, ALU.is_gt), t_cum[-1])
            q = ps(lambda e: e.tensor_tensor(u, u, mk, ALU.mult), q, t_mk)
            q = ps(lambda e: e.tensor_scalar(sk, nb, 0.5, 0.25, ALU.mult, ALU.add), q)
            q = ps(lambda e: e.tensor_scalar(sk, sk, 8388608.0, None, ALU.add), q)
            q = ps(lambda e: e.tensor_scalar(sk, sk, -8388608.0, None, ALU.add), q)
            q = ps(lambda e: e.tensor_scalar(v, sk, -1.5, None, ALU.mult), q)
            q = ps(lambda e: e.tensor_tensor(a15, v, u, ALU.mult), q)
            q = ps(lambda e: e.tensor_scalar(hh, sk, 0.5, -NOMATCH, ALU.mult, ALU.add), q)
            q = ps(lambda e: e.tensor_tensor(hh, hh, u, ALU.mult), q)
            q = ps(lambda e: e.tensor_scalar(hh, hh, NOMATCH, None, ALU.add), q)
            t_abs = []
            for t in range(T):
                cu = CUM[:, t * N:t * N + N]
                t_abs.append(AC.do(lambda e, cu=cu, t=t: e.activation(cu, cu, ACT.Abs,
                                                                     bias=SK[:, 3, t:t + 1]), q))
            for _ in range(LAG):
                yield
            for t in range(T):
                cu = CUM[:, t * N:t * N + N]
                w = DV.do(lambda e, cu=cu, t=t: e.tensor_scalar(cu, cu, SK[:, 4, t:t + 1], None,
                                                                ALU.is_equal), t_abs[t])
                if t % 4 == 3:
                    yield
            tok["sk_read"] = t_rem = w
            nd = POS[:, b]
            for k in range(T):
                for ch in range(2):
                    bk = ring("S")

                    def score(e, bk=bk, k=k, ch=ch):
                        o = banks[bk]
                        for j in range(4):
                            t = 4 * ch + j
                            oj = o[:, j * P:j * P + P]
                            at = t * N + k * P
                            e.matmul(oj, NEI[:, at:at + P], CH[:, CH_ID, :], start=(j == 0),
                                     stop=False, skip_group_check=True)
                            e.matmul(oj, CUM[:, at:at + P], CH[:, CH_NEG, :], start=False,
                                     stop=False, skip_group_check=True)
                            if t == k:
                                e.matmul(oj, CH[:, CH_ID, :], CH[:, CH_ID, :], start=False,
                                         stop=False, skip_group_check=True)
                        return e.matmul(o[:, :], CH[:, CH_NEG, :],
                                        CUM[:, k * N + 512 * ch:k * N + 512 * ch + 512],
                                        start=False, stop=True, skip_group_check=True)
                    w = PE.do(score, t_rem, t_nei[-1], free[bk])
                    ndc = nd[:, k, 512 * ch:512 * ch + 512]
                    free[bk] = AC.do(lambda e, ndc=ndc, bk=bk: e.activation(ndc, banks[bk][:, :],
                                                                          ACT.Relu), w, tok.get("pos_read"))
                if k % 2 == 1:
                    yield
            tok["nei_read"] = w
            tok["nd", b] = free[bk]

        def places(g, b):
            sl = g % 2
            nd, t_nd = POS[:, b], tok["nd", b]
            for ch in range(2):
                bk = ring("S")
                cs = slice(512 * ch, 512 * ch + 512)

                def total(e, bk=bk, cs=cs):
                    for k in range(T):
                        m = e.matmul(banks[bk][:, :], CH[:, CH_ONE, :], nd[:, k, cs],
                                     start=(k == 0), stop=(k == T - 1))
                    return m
                w = PE.do(total, t_nd, free[bk])
                fl = FL[0:1, cs] if b == 0 else FLO[0:1, :]
                for i, (n0, n1, d) in enumerate(CLASSES):
                    lo, hi = max(n0 - 512 * ch, 0), min(n1 - 512 * ch, 512)
                    if lo < hi:
                        f = AC.do(lambda e, bk=bk, lo=lo, hi=hi, i=i, fl=fl: e.activation(
                            fl[:, lo:hi], banks[bk][0:1, lo:hi], ACT.Relu,
                            bias=CF[0:1, CF_CAP + i:CF_CAP + i + 1]), w, *tok.get("fl_read", ()),
                            tok.get("flo_read"))
                if b == 1:
                    f = PO.do(lambda e, cs=cs: e.tensor_tensor(FL[0:1, cs], FL[0:1, cs], FLO[0:1, :],
                                                               ALU.add), f)
                    tok["flo_read"] = f
                for q in range(3):
                    r = AC.do(lambda e, bk=bk, q=q: e.activation(
                        RQ[:, q, :], banks[bk][:, :], ACT.Abs, scale=TAUS[q],
                        bias=CF[:, CF_BIASQ + q:CF_BIASQ + q + 1]), w, tok.get("rq_read"))
                free[bk] = r
                for q in range(3):
                    r = AC.do(lambda e, q=q: e.activation(
                        RQ[:, q, :], RQ[:, q, :], ACT.Relu, scale=-WTS[q],
                        bias=CF[:, CF_WQ + q:CF_WQ + q + 1]), free[bk])
                co = COEF[:, sl, b, cs]
                r = PO.do(lambda e, co=co: e.tensor_tensor(co, RQ[:, 0, :], RQ[:, 1, :], ALU.add), r,
                          tok.get(("coef_read", sl)))
                r = PO.do(lambda e, co=co: e.tensor_tensor(co, co, RQ[:, 2, :], ALU.add), r)
                tok["rq_read"] = r
                tok["coef", sl, b] = r
                yield
            for k in reversed(range(T)):
                for ch in range(2):
                    bk = ring("S")
                    cs = slice(512 * ch, 512 * ch + 512)

                    def place(e, bk=bk, k=k, cs=cs):
                        for j in range(k + 1):
                            m = e.matmul(banks[bk][:, :], CH[:, CH_PRE if j == k else CH_ONE, :],
                                         nd[:, j, cs], start=(j == 0), stop=(j == k))
                        return m
                    w = PE.do(place, t_nd, free[bk])
                    free[bk] = AC.do(lambda e, k=k, cs=cs, bk=bk: e.activation(
                        nd[:, k, cs], banks[bk][:, :], ACT.Copy), w)
                if k % 2 == 0:
                    yield
            tok["pos", b] = free[bk]
            tok["flags"] = tok.get("flo_read")

        def prepare(g):
            t_cum, t_nei = [], []
            yield from first_layer(g, 0, t_cum, t_nei)
            yield from thin(g, 0, t_cum, t_nei)
            t_cum, t_nei = [], []
            yield from both(first_layer(g, 1, t_cum, t_nei), places(g, 0))
            second = iter([0])
            yield from both(thin(g, 1, t_cum, t_nei), (second_norm(g) for _ in second))
            yield from places(g, 1)
            tok["any"] = DV.do(lambda e: e.tensor_reduce(ANY[0:1, g:g + 1], FL[:, :], AX, ALU.add),
                               tok["flags"])

        def both(x, y):
            x, y = iter(x), iter(y)
            more = [x, y]
            while more:
                for z in list(more):
                    if next(z, more) is more:
                        more.remove(z)
                yield

        def turn(g):
            for hf in range(2):
                bk = ring("T")
                for j in range(4):
                    h1 = H1[:, 4 * hf + j].rearrange("p b c -> p (b c)")
                    tp = PE.do(lambda e, bk=bk, j=j, h1=h1: e.transpose(
                        banks[bk][:, j * P:j * P + P], h1, idf), tok["h1"], free[bk] if j == 0 else None)
                free[bk] = AC.do(lambda e, bk=bk, hf=hf: e.activation(
                    H1T[:, 512 * hf:512 * hf + 512], banks[bk][:, :], ACT.Copy), tp, tok.get("h1t_read"))
            tok["h1_read"] = tp
            tok["h1t"] = free[bk]

        def overflow(g, my):
            g0, g1 = banks["G0"], banks["G1"]
            any_ap = ANY[0:1, g:g + 1].bitcast(I32)
            fl_ap = FL[0:1, :].bitcast(I32)
            room = OHB[:, 0:6 * 2 * N].bitcast(F32).rearrange("p (i n) -> p i n", n=N)
            va, vb, wt, io, u, u2 = (room[:, i, :] for i in range(6))

            def on_pe(e):
                flag = e.value_load(any_ap)
                with e.If(flag):
                    with e.Fori(0, N // 2) as i:
                        f = e.value_load(fl_ap[:, bass.ds(i, 1)])
                        with e.If(f):
                            for _ in range(2):
                                e.wait_ge(f_d, 1)
                                e.sem_clear(f_d)
                                for k in range(T):
                                    gb = (g0, g1)[k // 4]
                                    for b in range(2):
                                        mm = e.matmul(gb[C * b:C * b + C, (k % 4) * P:(k % 4) * P + P],
                                                      COL[:, b, k, :].to_broadcast([P, C]),
                                                      CH[:, CH_ID, :], start=(k % 4 == 0),
                                                      stop=(k % 4 == 3), skip_group_check=True)
                                mm.then_inc(f_p, 1)
                return e.sem_inc(f_e, 1)

            def on_dve(e):
                def link(ins):
                    ins.then_inc(f_l, 1)
                    e.wait_ge(f_l, 1)
                    e.sem_clear(f_l)

                flag = e.value_load(any_ap)
                with e.If(flag):
                    link(e.memset(ZF[:, :], -BIG))
                    link(e.memset(u, 1.0))
                    link(e.tensor_tensor_scan(io, u, u, 0.0, ALU.add, ALU.max))
                    with e.Fori(0, N // 2) as i:
                        f = e.value_load(fl_ap[:, bass.ds(i, 1)])
                        with e.If(f):
                            for odd in range(2):
                                for b in range(2):
                                    link(e.tensor_copy(COL[:, b], POS[:, b, :, bass.ds(i * 2 + odd, 1)]))
                                e.sem_inc(f_d, 1)
                                e.wait_ge(f_p, 1)
                                e.sem_clear(f_p)
                                for j, gb in enumerate((g0, g1)):
                                    link(e.tensor_scalar(va[:, 512 * j:512 * j + 512], gb[:, :], 1024.5,
                                                         BIG, ALU.is_lt, ALU.mult))
                                link(e.tensor_scalar(u, va, 0.5 * BIG, None, ALU.is_gt))
                                link(e.tensor_reduce(FB[:, 3:4], u, AX, ALU.add))
                                link(e.tensor_scalar(FB[:, 0:1], FB[:, 3:4], -1.0, float(N), ALU.mult,
                                                     ALU.add))
                                link(e.tensor_tensor(va, va, H1T[:, :], ALU.max))
                                cur, nxt = va, vb
                                for p, k in merge_stages(N):
                                    c3 = cur.rearrange("q (n o) -> q n o", o=1)
                                    n3 = nxt.rearrange("q (n o) -> q n o", o=1)
                                    a0, a1, ar = stage_views(c3, p, k)
                                    b0, b1, br = stage_views(n3, p, k)
                                    link(e.tensor_tensor(b0, a0, a1, ALU.min))
                                    link(e.tensor_tensor(b1, a0, a1, ALU.max))
                                    if ar is not None:
                                        link(e.tensor_copy(br, ar))
                                    cur, nxt = nxt, cur
                                nv = FB[:, 0:1]
                                link(e.memset(wt, 0.0))
                                for q in range(3):
                                    link(e.tensor_scalar(FB[:, 1:2], nv, TAUS[q], 1.0 - TAUS[q],
                                                         ALU.mult, ALU.add))
                                    link(e.tensor_scalar(u, io, FB[:, 1:2], None, ALU.subtract))
                                    link(e.tensor_scalar(u2, u, -1.0, None, ALU.mult))
                                    link(e.tensor_tensor(u, u, u2, ALU.min))
                                    link(e.tensor_scalar(u, u, 1.0, 0.0, ALU.add, ALU.max))
                                    link(e.scalar_tensor_tensor(out=wt, in0=u, scalar=WTS[q], in1=wt,
                                                                op0=ALU.mult, op1=ALU.add))
                                link(e.tensor_tensor(nxt, cur, wt, ALU.mult))
                                link(e.tensor_reduce(FB[:, 2:3], nxt, AX, ALU.add))
                                link(e.tensor_tensor(ZF[:, bass.ds(i * 2 + odd, 1)], FB[:, 2:3],
                                                     H1T[:, bass.ds(i * 2 + odd, 1)], ALU.add))
                return e.memset(MARK[:, :], 0.0)

            PE.do(on_pe, tok["any"], tok["pos", 0], tok["pos", 1], free["G0"], free["G1"], c_all)
            tok["mark"] = DV.do(on_dve, tok["any"], tok["h1t"], tok.get("mark"), tok["oh_last"])
            tok["fl_read"] = (tok["mark"], DmaToken(f_e, g + 1))
            tok["pos_read"] = tok["nei_read"] = tok["mark"]
            free["G0"] = free["G1"] = tok["mark"]

        def chunks_of(ci):
            n0, n1, d = CLASSES[ci]
            w = n1 - n0
            if ci == 3:
                return [(0, 512, j, 1) for j in range(d)] + [(512, 256, j, min(2, d - j)) for j in range(0, d, 2)]
            per = 512 // w
            return [(0, w, j, min(per, d - j)) for j in range(0, d, per)]

        class Chunk:
            pass

        def gather(ci, lane0, w, d0, nd, my):
            n0 = CLASSES[ci][0] + lane0
            c = Chunk()
            c.cols = w * nd
            r = st["OH"] = (st.get("OH", -1) + 1) % 2
            c.bk = ring("G")
            bk = c.bk
            ohs = []
            for b in range(2):
                oh = OHB[:, (2 * r + b) * 4096:(2 * r + b) * 4096 + T * c.cols]\
                    .rearrange("p (k c) -> p k c", k=T)
                ps = POS[:, b, :, n0:n0 + w]
                waits = (tok["pos", b], oh_free[r], tok["nei_read"])
                if ci == 0:
                    for k4 in range(2):
                        ov = oh[:, 4 * k4:4 * k4 + 4, :].rearrange("p k (d n) -> p k d n", n=w)
                        pv = ps[:, 4 * k4:4 * k4 + 4, :].unsqueeze(2).to_broadcast([P, 4, nd, w])
                        iv = CH[:, CH_IOTA, d0:d0 + nd].unsqueeze(1).unsqueeze(3)\
                            .to_broadcast([P, 4, nd, w])
                        for kk in range(4):
                            t = DV.do(lambda e, ov=ov, pv=pv, iv=iv, kk=kk: e.tensor_tensor(
                                ov[:, kk], pv[:, kk], iv[:, kk], ALU.is_equal), *waits, c_all)
                else:
                    for j in range(nd):
                        t = DV.do(lambda e, oh=oh, ps=ps, j=j, d=d0 + j, w=w: e.tensor_scalar(
                            oh[:, :, j * w:j * w + w], ps, float(N + 1 + d), None, ALU.is_equal), *waits)
                ohs.append(oh)
            def mms(e):
                for k in range(T):
                    for part in range(2):
                        for b in range(2):
                            m = e.matmul(banks[bk][C * b:C * b + C, 0:c.cols], HL[:, part, b, k, :],
                                         ohs[b][:, k, :], start=(k == 0 and part == 0),
                                         stop=(k == T - 1 and part == 1), skip_group_check=True)
                return m
            c.mm = PE.do(mms, t, tok["hl"], free[bk])
            oh_free[r] = c.mm
            tok["oh_last"] = c.mm
            c.args = (ci, lane0, w, d0, nd)
            return c

        def gather_all(ci, put, my, *waits):
            for a in chunks_of(ci):
                c = gather(ci, *a, my)
                for dst, src in put(c.cols, *a):
                    t = AC.do(lambda e, dst=dst, src=src, bk=c.bk: e.activation(
                        dst, banks[bk][:, src], ACT.Copy), c.mm, *waits)
                free[c.bk] = t
                yield
            my["ev", ci] = t

        def batcher(ci, my):
            n0, n1, d = CLASSES[ci]
            w = n1 - n0
            cur, nxt = (v[:, 0:d * w].rearrange("p (d n) -> p d n", n=w) for v in (SZ if ci == 0 else SA, SB))
            t = my["ev", ci]
            for p, k in merge_stages(d):
                a0, a1, ar = stage_views(cur, p, k)
                b0, b1, br = stage_views(nxt, p, k)
                wb = (t, tok.get("sb_read"))
                t = DV.do(lambda e, b0=b0, a0=a0, a1=a1: e.tensor_tensor(b0, a0, a1, ALU.max), *wb)
                t = DV.do(lambda e, b1=b1, a0=a0, a1=a1: e.tensor_tensor(b1, a0, a1, ALU.min), *wb)
                if ar is not None:
                    t = DV.do(lambda e, br=br, ar=ar: e.tensor_copy(br, ar), *wb)
                cur, nxt = nxt, cur
                yield
            tok["sb_read"] = t
            my["sorted", ci] = (cur, t)

        def coef_rows(my, ci, lane0, w, d0, nd):
            n0 = CLASSES[ci][0] + lane0
            bk = ring("G")
            co = COEF[:, my["sl"]]

            def mms(e):
                oo = [banks[bk][C * b:C * b + C, 0:w * nd] for b in range(2)]
                if ci == 0:
                    ov = [o.rearrange("p (d n) -> p d n", n=w) for o in oo]
                    for n in range(w):
                        for b in range(2):
                            m = e.matmul(ov[b][:, :, n], co[:, b, n0 + n:n0 + n + 1].to_broadcast([P, C]),
                                         CH[:, CH_SEL, d0:d0 + nd], start=(n == 0), stop=(n == w - 1),
                                         skip_group_check=True)
                else:
                    for j in range(nd):
                        for b in range(2):
                            m = e.matmul(oo[b][:, j * w:j * w + w],
                                         CH[:, CH_SEL, d0 + j:d0 + j + 1].to_broadcast([P, C]),
                                         co[:, b, n0:n0 + w], start=(j == 0), stop=(j == nd - 1),
                                         skip_group_check=True)
                return m
            t = PE.do(mms, tok["coef", my["sl"], 0], tok["coef", my["sl"], 1], free[bk], c_all)
            tok["coef_read", my["sl"]] = t
            return bk, t

        def weigh(ci, my):
            n0, n1, d = CLASSES[ci]
            w = n1 - n0
            cur, t = my["sorted", ci]
            flat = cur.rearrange("p d n -> p (d n)")
            for lane0, w_, d0, nd in chunks_of(ci):
                bk, mm = coef_rows(my, ci, lane0, w_, d0, nd)
                v = flat[:, d0 * w:(d0 + nd) * w]
                t = DV.do(lambda e, v=v, bk=bk, n=nd * w: e.tensor_tensor(v, v, banks[bk][:, 0:n], ALU.mult),
                          t, mm)
                free[bk] = t
                yield
            r = DV.do(lambda e: e.tensor_reduce(RED[:, n0:n1], cur.rearrange("p d n -> p n d"), AX, ALU.add),
                      t, tok.get("red_read"))
            if ci == 1:
                tok["sb_read"] = r
            my["red", ci] = r
            yield

        def network(my):
            loc = list(range(11))
            spare = [(i, None) for i in range(11, NSL)]
            layer = my["ev", 3]
            for level in NET11:
                t = None
                for i, j in level:
                    (la, lb) = loc[i], loc[j]
                    (s1, r1), (s2, r2) = spare.pop(0), spare.pop(0)
                    DV.do(lambda e, la=la, lb=lb, s1=s1: e.tensor_tensor(SL[:, s1, :], SL[:, la, :],
                                                                        SL[:, lb, :], ALU.max), layer, r1)
                    t = DV.do(lambda e, la=la, lb=lb, s2=s2: e.tensor_tensor(SL[:, s2, :], SL[:, la, :],
                                                                            SL[:, lb, :], ALU.min), layer, r2)
                    loc[i], loc[j] = s1, s2
                    spare += [(la, t), (lb, t)]
                    yield
                layer = t
            my["sorted", 3] = (loc, layer)
            my["spare"] = [a for a, _ in spare]

        def weigh_last(my):
            loc, t = my["sorted", 3]
            done = {}
            for lane0, w, d0, nd in chunks_of(3):
                bk, mm = coef_rows(my, 3, lane0, w, d0, nd)
                for j in range(nd):
                    v = SL[:, loc[d0 + j], lane0:lane0 + w]
                    t = DV.do(lambda e, v=v, bk=bk, j=j, w=w: e.tensor_tensor(
                        v, v, banks[bk][:, j * w:j * w + w], ALU.mult), my["sorted", 3][1], mm)
                    d = d0 + j
                    s_ = PE.do(lambda e, v=v, d=d, w=w: e.matmul(
                        banks["M"][:, 0:w], idf, v, start=(d == 0), stop=(d == 10)), t,
                        free["M"] if d == 0 else None)
                free[bk] = t
                yield
                if d0 + nd == 11:
                    z = my["z"]
                    for n in range(256 + lane0, 256 + lane0 + w, 256):
                        zc = z[n // 512][:, n % 512:n % 512 + 256]
                        t = DV.do(lambda e, zc=zc, n=n, lane0=lane0: e.tensor_tensor(
                            zc, banks["M"][:, n - 256 - lane0:n - lane0], H1T[:, n:n + 256], ALU.add), s_)
                    free["M"] = t
                    yield
            my["z1"] = t

        def finish(g, my):
            sl = g % 2
            sp = my["spare"]
            z = my["z"]
            hid = [SL[:, sp[2], 0:512], SZ[:, 0:512]]
            tmp = SL[:, sp[3], 0:512]
            t = DV.do(lambda e: e.tensor_tensor(z[0][:, 0:256], RED[:, :], H1T[:, 0:256], ALU.add),
                      my["red", 0], my["red", 1], my["red", 2], my["sorted", 3][1])
            tok["red_read"] = t
            any_ap = ANY[0:1, g:g + 1].bitcast(I32)

            def patch(e):
                def link(ins):
                    ins.then_inc(f_l, 1)
                    e.wait_ge(f_l, 1)
                    e.sem_clear(f_l)

                flag = e.value_load(any_ap)
                with e.If(flag):
                    for ch in range(2):
                        mask = tmp.bitcast(I32)
                        zf = ZF[:, 512 * ch:512 * ch + 512]
                        link(e.tensor_scalar(mask, zf, -0.5 * BIG, None, ALU.is_gt))
                        link(e.copy_predicated(z[ch], mask, zf))
                return e.memset(MARK[:, :], 0.0)
            t = tok["mark"] = DV.do(patch, t, my["z1"], tok["mark"])
            tok["h1t_read"] = t
            t_z = t
            yield
            hr = [None, None]
            for b in range(2):
                bm = "M"
                for ch in range(2):
                    bk = ring("S")
                    w = PE.do(lambda e, b=b, ch=ch, bk=bk: e.matmul(
                        banks[bk][:, :], W1[C * b:C * b + C, :], z[ch][C * b:C * b + C, :], start=True,
                        stop=True), t_z, free[bk])
                    a = AC.do(lambda e, bk=bk, ch=ch: e.activation(hid[ch], banks[bk][:, :], ACT.Relu,
                                                                  bias=B1[:, 0:1]), w, hr[ch], t_z)
                    free[bk] = a

                    def second(e, ch=ch, bm=bm):
                        for j in range(4):
                            o = banks[bm][:, (4 * ch + j) * C:(4 * ch + j) * C + C]
                            e.matmul(o, hid[ch][:, j * P:j * P + P], W2[:, :], start=(ch == 0 and j == 0),
                                     stop=False, skip_group_check=True)
                            m = e.matmul(o, CF[0:1, CF_ONE:CF_ONE + P], B2[0:1, :], start=False,
                                         stop=(ch == 1 and j == 3), skip_group_check=True)
                        return m
                    y = PE.do(second, a, free[bm])
                    hr[ch] = y
                mk = MK[:, (2 * g + b) * T:(2 * g + b) * T + T].unsqueeze(2).to_broadcast([P, T, C])
                tv = tmp.rearrange("p (t c) -> p t c", c=C)
                t = DV.do(lambda e, tv=tv, mk=mk, bm=bm: e.tensor_tensor(
                    tv, banks[bm][:, :].rearrange("p (t c) -> p t c", c=C), mk, ALU.mult), y,
                    tok.get("tmp_read"), t_z)
                free[bm] = t
                xv = X[:, sl, b]
                t = PO.do(lambda e, tv=tv, xv=xv: e.tensor_tensor(xv, xv, tv, ALU.add), t)
                tok["tmp_read"] = t
                out_n[sl] += 16
                x_free[sl] = dma(out_d[2 * g + b].rearrange("(t p) c -> p t c", p=P), xv, s_out[sl],
                                 out_n[sl], t)
                yield
            tok["sl_read"] = (t, y)

        def together(*gens):
            total = max(n for n, _ in gens)
            done = [0] * len(gens)
            for i in range(total):
                for j, (n, gen) in enumerate(gens):
                    while done[j] * total < (i + 1) * n:
                        next(gen, None)
                        done[j] += 1
            for _, gen in gens:
                for _ in gen:
                    pass

        def chain(*gens):
            for gen in gens:
                yield from gen

        load_x(0)
        load_x(1)
        first_norm(0)
        together((1, prepare(0)))
        turn(0)
        for g in range(NP):
            my = {"sl": g % 2}

            def put(buf):
                def places(cols, lane0, w, d0, nd):
                    yield buf[:, d0 * w:d0 * w + cols], slice(0, cols)
                return places

            def put_last(cols, lane0, w, d0, nd):
                for j in range(nd):
                    yield SL[:, d0 + j, lane0:lane0 + w], slice(j * w, j * w + w)

            later = tok.get("sl_read", ())
            c3 = gather_all(3, put_last, my, *later)
            for _ in chain(gather_all(0, put(SZ), my, *later),
                           gather_all(1, put(SA), my, tok.get("sa_read"))):
                pass
            together((17, c3), (52, chain(batcher(0, my), batcher(1, my), weigh(0, my), weigh(1, my))))
            net = network(my)
            if g + 1 < NP:
                first_norm(g + 1)
            together((8, gather_all(2, put(SA), my, my["sorted", 1][1])),
                     (EARLY, itertools.islice(net, EARLY)))
            tok["oh_read"] = tok["oh_last"]
            overflow(g, my)

            def tail():
                yield from batcher(2, my)
                yield from weigh(2, my)
                tok["sa_read"] = my["red", 2]
                yield from net
                sp = my["spare"]
                my["z"] = [SL[:, sp[0], 0:512], SL[:, sp[1], 0:512]]
                yield from weigh_last(my)
                yield from finish(g, my)
            if g + 1 < NP:
                together((68, tail()), (PREP, prepare(g + 1)))
                turn(g + 1)
                if g + 2 < NP:
                    load_x(g + 2)
            else:
                together((1, tail()))

        for lane in (PE, AC, DV, PO, SP):
            lane.count()
        block = ctx.enter_context(nc.Block())

        @block.tensor
        def _(e):
            PE.issue(e)

        @block.scalar
        def _(e):
            AC.issue(e)

        @block.vector
        def _(e):
            DV.issue(e)

        @block.gpsimd
        def _(e):
            PO.issue(e)

        @block.sync
        def _(e):
            SP.issue(e)
            for i in range(2):
                e.wait_ge(s_out[i], out_n[i])


def constants():
    import numpy as np

    cf = np.zeros((P, CF_N), np.float32)
    cf[:, CF_ID:CF_ID + P] = np.eye(P)
    d = np.arange(P)
    for q in range(3):
        cf[:, CF_BIASQ + q] = -(TAUS[q] + d)
        cf[:, CF_WQ + q] = WTS[q]
    cf[:, CF_EPS] = 1e-5
    for i, (_, _, slots) in enumerate(CLASSES):
        cf[:, CF_CAP + i] = -slots
    cf[:, CF_ONE:CF_ONE + P] = 1.0
    ch = np.zeros((P, 7, P), np.float16)
    ch[:, CH_ID] = np.eye(P)
    ch[:, CH_NEG] = -np.eye(P)
    ch[:, CH_PRE] = np.triu(np.ones((P, P))) + N * np.eye(P)
    ch[:, CH_ONE] = 1.0
    ch[:, CH_OFF] = 1.0 - np.eye(P)
    ch[:, CH_IOTA] = N + 1 + d[None, :]
    ch[:, CH_SEL] = np.eye(P) / HSCALE
    return cf, ch


def kernel(x, adj, nodemask, L1_gnn_W1, L1_gnn_b1, L1_gnn_W2, L1_gnn_b2):
    import numpy as np
    import concourse.bacc as bacc
    from concourse.bass_utils import run_bass_kernel_spmd

    nc = bacc.Bacc("TRN2", target_bir_lowering=False, num_devices=1)
    cf, ch = constants()
    given = {
        "x": x, "adj": adj, "nodemask": np.ascontiguousarray(nodemask).view(np.uint8), "w1": L1_gnn_W1,
        "b1": L1_gnn_b1, "w2": L1_gnn_W2, "b2": L1_gnn_b2, "cf": cf, "ch": ch,
    }
    arrays, args = {}, []
    for name, a in given.items():
        a = np.ascontiguousarray(a)
        arrays[f"in_{name}"] = a
        args.append(nc.dram_tensor(f"in_{name}", a.shape, mybir.dt.from_np(a.dtype),
                                   kind="ExternalInput").ap())
    out = nc.dram_tensor("out_0", (B, N, C), F32, kind="ExternalOutput").ap()
    program(nc, *args, out)
    r = run_bass_kernel_spmd(nc, [arrays], core_ids=[0])
    return r.results[0]["out_0"]
```

```python
import itertools
from contextlib import ExitStack

import concourse.bass as bass
from concourse import mybir

ALU = mybir.AluOpType
ACT = mybir.ActivationFunctionType
F32 = mybir.dt.float32
F16 = mybir.dt.float16
I32 = mybir.dt.int32
AX = mybir.AxisListType.X

B, N, C, H = 16, 1024, 64, 128
P = 128
T = N // P
NP = B // 2
TAUS = (0.25, 0.5, 0.75)
WTS = (0.25, 0.5, 0.25)
HSCALE = 4096.0
BIG = 1.0e9
NOMATCH = 9999.0
COLS = 512
EARLY, IDLE, SPLIT = 90, 20, 7
LAG, REST, PAUSE, CLAG, PRE, STORE = 2, 8, 1, 1, 8, 10

CLASSES = [(0, 8, 128), (8, 88, 32), (88, 256, 16), (256, 1024, 11)]
THIRD = 256
HUBS, HUB_LANES = 2, 10
HUB_PARTS = [(0, HUBS, 0, 128), (HUBS, 8 - HUBS, 0, 64)]
CAPS = [(0, HUBS, 128), (HUBS, 8, 64)] + CLASSES[1:]
NET11 = [
    [(0, 9), (1, 6), (2, 4), (3, 7), (5, 8)],
    [(0, 1), (3, 5), (4, 10), (6, 9), (7, 8)],
    [(1, 3), (2, 5), (4, 7), (8, 10)],
    [(0, 4), (1, 2), (3, 7), (5, 9), (6, 8)],
    [(0, 1), (2, 6), (4, 5), (7, 8), (9, 10)],
    [(2, 4), (3, 6), (5, 7), (8, 9)],
    [(1, 2), (3, 4), (5, 6), (7, 8)],
    [(2, 3), (4, 5), (6, 7)],
]

CF_ID, CF_BIASQ, CF_WQ, CF_EPS, CF_CAP, CF_ONE, CF_N = 0, 128, 131, 134, 135, 140, 268
(CH_ID, CH_NEG, CH_PRE, CH_ONE, CH_OFF, CH_IOTA, CH_SEL) = range(7)


class Token:

    def __init__(self, lane):
        self.lane, self.used, self.value = lane, False, None


class DmaToken:
    def __init__(self, sem, value):
        self.sem, self.value, self.used = sem, value, True


class Lane:

    def __init__(self, sem):
        self.sem, self.ops = sem, []

    def do(self, fn, *waits):
        t = Token(self)
        for w in waits:
            if w is not None:
                w.used = True
        self.ops.append((fn, [w for w in waits if w is not None], t))
        return t

    def count(self):
        n = 0
        for _, _, t in self.ops:
            if t.used:
                n += 1
                t.value = n

    def issue(self, eng):
        seen = {}
        for fn, waits, t in self.ops:
            for w in waits:
                sem = w.sem if isinstance(w, DmaToken) else w.lane.sem
                if seen.get(id(sem), 0) < w.value:
                    eng.wait_ge(sem, w.value)
                    seen[id(sem)] = w.value
            ins = fn(eng)
            if t.used:
                ins.then_inc(self.sem, 1)


def merge_stages(n):
    p = 1
    while p < n:
        k = p
        while k >= 1:
            yield p, k
            k //= 2
        p *= 2


def stage_views(x, p, k):
    if k == p:
        v = x.rearrange("q (b h p) n -> q b h (p n)", h=2, p=p)
        return v[:, :, 0, :], v[:, :, 1, :], None
    c = 2 * p // k
    v = x.rearrange("q (b c k) n -> q b c (k n)", c=c, k=k)
    return v[:, :, 1:c - 1:2, :], v[:, :, 2:c:2, :], v[:, :, 0:c:c - 1, :]


def program(nc, x_d, adj_d, mask_d, w1_d, b1_d, w2_d, b2_d, cf_d, ch_d, out_d):
    with ExitStack() as ctx:
        def sb(name, shape, dt=F32):
            return ctx.enter_context(nc.sbuf_tensor(name, shape, dt))

        def sem(name):
            return ctx.enter_context(nc.semaphore(name))

        banks = {k: ctx.enter_context(nc.psum_tensor("ps" + k, [P, 512], F32))
                 for k in ("T0", "T1", "L", "S0", "S1", "G0", "G1", "M")}

        X = sb("X", [P, 3, 2, T, C])
        H0A = sb("H0A", [P, 2 * T, C + 1])
        XC = sb("XC", [P, 2 * T, C])
        H1 = sb("H1", [P, T, 2, C])
        HL = sb("HL", [P, 2, 2, T, C], F16)
        NADJ = 2
        ADJ = sb("ADJ", [P, NADJ, N])
        ADJT = sb("ADJT", [P, 2, 4, P])
        OHB = sb("OHB", [P, 2 * T * COLS], F16)
        NEI = sb("NEI", [P, T * N], F16)
        CUM = sb("CUM", [P, T * N], F16)
        POS = sb("POS", [P, 3, T, N], F16)
        NSL = 15
        SL = sb("SL", [P, NSL, THIRD])
        SA = sb("SA", [P, 16 * 168])
        SB = sb("SB", [P, 16 * 168])
        RED = sb("RED", [P, 256])
        SZ = sb("SZ", [P, 1024])
        COEF = sb("COEF", [P, 2, 2, N], F16)
        RQ = sb("RQ", [P, 2, 256], F16)
        Z = sb("Z", [P, N])
        HUB = sb("HUB", [P, 2, T, HUB_LANES], F16)
        H1T = sb("H1T", [P, N])
        ZF = sb("ZF", [P, N])
        FL = sb("FL", [1, N], F16)
        FLO = sb("FLO", [1, N], F16)
        ANY = sb("ANY", [1, NP])
        CF = sb("CF", [P, CF_N])
        CH = sb("CH", [P, 7, P], F16)
        W1 = sb("W1", [P, H])
        W2 = sb("W2", [P, C])
        B1 = sb("B1", [P, 1])
        B2 = sb("B2", [1, C])
        MU8 = sb("MU8", [P, P], mybir.dt.uint8)
        MKF = SL[:, 0, 0:128]
        MK = sb("MK", [P, B * T])
        ST = sb("ST", [P, 6, 2 * T])
        SK = sb("SK", [P, 8, T])
        FB = sb("FB", [P, 4])
        MARK = sb("MARK", [P, 1])
        COL = sb("COL", [P, 2, T, 1], F16)

        s = {k: sem("s_" + k) for k in ("pe", "act", "dve", "pool", "sp")}
        PE, AC, DV, PO, SP = (Lane(s[k]) for k in ("pe", "act", "dve", "pool", "sp"))
        s_adj = [sem(f"s_adj{i}") for i in range(NADJ)]
        s_x = [sem(f"s_x{i}") for i in range(3)]
        s_out = [sem(f"s_out{i}") for i in range(3)]
        s_c = sem("s_c")
        f_p, f_d, f_l, f_e = sem("f_p"), sem("f_d"), sem("f_l"), sem("f_e")

        idf = CF[:, CF_ID:CF_ID + P]

        def dma(dst, src, sm, value, *waits):
            SP.do(lambda e: Done(e.dma_start(dst, src).then_inc(sm, 16)), *waits)
            return DmaToken(sm, value)

        class Done:

            def __init__(self, ins):
                self.ins = ins

        n_c = 0

        def const(dst, src):
            nonlocal n_c
            n_c += 16
            return dma(dst, src, s_c, n_c)

        const(CF[:, :], cf_d)
        const(CH[:, :, :], ch_d)
        const(W1[0:C, :], w1_d)
        const(W1[C:P, :], w1_d)
        const(W2[:, :], w2_d)
        const(B1[:, :], b1_d.rearrange("(h o) -> h o", o=1))
        const(B2[:, :], b2_d.rearrange("(o c) -> o c", o=1))
        c_all = const(MU8[:, :], mask_d.rearrange("b (t p) -> (b t) p", p=P))
        t_one = DV.do(lambda e: e.memset(H0A[:, :, C:C + 1], 1.0))
        t = DV.do(lambda e: e.tensor_copy(MKF, MU8[:, :]), c_all)
        t = PE.do(lambda e: e.transpose(banks["M"][:, 0:P], MKF, idf), t, c_all)
        t_mk = DV.do(lambda e: e.tensor_copy(MK[:, :], banks["M"][:, 0:P]), t)
        free = {k: None for k in banks}
        free["M"] = t_mk

        adj_n, adj_free = 0, [None] * NADJ
        at_free = [None, None]
        st = {"T": 0, "S": 0, "G": 0, "AT": 0}

        def ring(kind):
            k = f"{kind}{st[kind] % 2}"
            st[kind] += 1
            return k

        tok = {}
        oh_free = [None, None]
        x_ready, x_free = {}, {}
        out_n = [0] * 3

        def layernorm_relu(src, outs, waits, tag):
            sums, mean, var, sd, rs = (ST[:, i, :] for i in range(5))
            bc = lambda v: v.unsqueeze(2).to_broadcast([P, 2 * T, C])
            sq = H0A[:, :, 0:C] if tag == 0 else H1[:, :, :, :].rearrange("p t b c -> p (t b) c")
            a = DV.do(lambda e: e.tensor_reduce(sums, src, AX, ALU.add), *waits)
            a = DV.do(lambda e: e.tensor_scalar(mean, sums, 1.0 / C, None, ALU.mult), a)
            a = DV.do(lambda e: e.tensor_tensor(XC[:, :, :], src, bc(mean), ALU.subtract), a)
            a = DV.do(lambda e: e.tensor_tensor(sq, XC[:, :, :], XC[:, :, :], ALU.mult), a)
            a = DV.do(lambda e: e.tensor_reduce(var, sq, AX, ALU.add), a)
            a = AC.do(lambda e: e.activation(sd, var, ACT.Sqrt, bias=CF[:, CF_EPS:CF_EPS + 1],
                                             scale=1.0 / C), a, c_all)
            a = DV.do(lambda e: e.reciprocal(rs, sd), a)
            for i, o in enumerate(outs):
                r = ST[:, 4, T * i:T * i + T].unsqueeze(2).to_broadcast([P, T, C])
                xc = XC[:, T * i:T * i + T, :]
                last = DV.do(lambda e, o=o, r=r, xc=xc: e.scalar_tensor_tensor(
                    out=o, in0=xc, scalar=0.0, in1=r, op0=ALU.max, op1=ALU.mult), a)
            return last

        def load_x(g):
            sl = g % 3
            t = None
            for i in range(2):
                t = dma(X[:, sl, i], x_d[2 * g + i].rearrange("(t p) c -> p t c", p=P), s_x[sl],
                        32 * (g // 3) + 16 * (i + 1), x_free.get(sl))
            x_ready[g] = t

        def first_norm(g):
            xs = X[:, g % 3].rearrange("p b t c -> p (b t) c")
            tok["h0"] = layernorm_relu(xs, [H0A[:, T * i:T * i + T, 0:C] for i in range(2)],
                                       [x_ready[g], t_one, tok.get("h0_read"), tok.get("xc_read")], 0)

        def second_norm(g):
            xs = X[:, g % 3].rearrange("p b t c -> p (b t) c")
            t_h1 = layernorm_relu(xs, [H1[:, :, i, :] for i in range(2)],
                                  [tok["x1"], tok.get("h1_read")], 1)
            tok["xc_read"] = tok["h1"] = t_h1

        def halves(g):
            t_h1 = tok["h1"]
            for i in range(2):
                h1, hi, lo = H1[:, :, i, :], HL[:, 0, i], HL[:, 1, i]
                w = AC.do(lambda e, h1=h1, hi=hi: e.activation(hi, h1, ACT.Copy, scale=HSCALE), t_h1,
                          tok.get("oh_read"))
                w = DV.do(lambda e, h1=h1, hi=hi, lo=lo: e.scalar_tensor_tensor(
                    out=lo, in0=h1, scalar=HSCALE, in1=hi, op0=ALU.mult, op1=ALU.subtract), w)
            tok["hl"] = w

        def first_layer(g, b, t_cum, t_nei):
            nonlocal adj_n
            sl = g % 3
            late, results, counts = [], [], []

            def messages(t, hf, i2, ev):
                for j in range(4):
                    kt = 4 * hf + j
                    mm = PE.do(lambda e, j=j, kt=kt: e.matmul(
                        banks["L"][:, 65 * (t % 4):65 * (t % 4) + 65], ADJT[:, i2, j, :],
                        H0A[:, T * b + kt, :], start=(kt == 0), stop=(kt == T - 1),
                        skip_group_check=True),
                        ev if j == 0 else None, tok["h0"], free["L"] if t % 4 == 0 else None)
                at_free[i2] = mm
                if b == 1 and t == T - 1:
                    tok["h0_read"] = mm
                if t % 4 == 3 and hf == 1:
                    results.append((t - 3, mm))

            def result(t0, mm):
                lv = banks["L"][:, 0:260].rearrange("p (t c) -> p t c", c=65)
                dg = ST[:, 5, 4 * (t0 // 4):4 * (t0 // 4) + 4]
                q = DV.do(lambda e: e.tensor_scalar(dg, lv[:, :, 64], 1.0, None, ALU.max), mm,
                          tok.get("dg_read"))
                q = DV.do(lambda e: e.reciprocal(dg, dg), q)
                msg = XC[:, T * b + t0:T * b + t0 + 4, :]
                q = DV.do(lambda e: e.tensor_tensor(
                    msg, lv[:, :, 0:64], dg.unsqueeze(2).to_broadcast([P, 4, C]), ALU.mult),
                    q, tok["h0"])
                free["L"] = tok["dg_read"] = q
                xv = X[:, sl, b, t0:t0 + 4, :]
                tok["x1"] = PO.do(lambda e: e.tensor_tensor(xv, xv, msg, ALU.add), q)

            def count(t, cu, nei, d2, before):
                d3 = DV.do(lambda e: e.tensor_tensor_scan(cu, nei, nei, 0.0, ALU.add, ALU.max), d2, before)
                d3 = PO.do(lambda e: e.tensor_copy(SK[:, 0, t:t + 1], cu[:, N - 1:N]), d3,
                           tok.get("sk_read"))
                t_cum.append(PO.do(lambda e: e.tensor_tensor(cu, cu, nei, ALU.mult), d3))

            for t in range(T):
                k = adj_n % NADJ
                adj_n += 1
                a = ADJ[:, k, :]
                got = dma(a, adj_d[2 * g + b, t * P:t * P + P, :], s_adj[k],
                          16 * ((adj_n - 1) // NADJ + 1), *(adj_free[k] or ()))
                nei = NEI[:, t * N:t * N + N]
                nd0 = nei[:, t * P:t * P + P]
                before = tok.get("nei_read")
                d = AC.do(lambda e, nei=nei, a=a: e.activation(nei, a, ACT.Sign), got, before)
                d2 = AC.do(lambda e, nei=nei: e.activation(nei, nei, ACT.Relu), d)
                d2 = PO.do(lambda e, nd0=nd0: e.tensor_tensor(nd0, nd0, CH[:, CH_OFF, :], ALU.mult),
                           d2, c_all)
                t_nei.append(d2)
                cu = CUM[:, t * N:t * N + N]
                counts.append((t, cu, nei, d2, before))
                if len(counts) > CLAG:
                    count(*counts.pop(0))
                for hf in range(2):
                    if results:
                        result(*results.pop())
                    bk = ring("T")
                    for j in range(4):
                        c0 = (4 * hf + j) * P
                        tp = PE.do(lambda e, bk=bk, j=j, a=a, c0=c0: e.transpose(
                            banks[bk][:, j * P:j * P + P], a[:, c0:c0 + P], idf),
                            got, c_all, free[bk] if j == 0 else None)
                    if late:
                        messages(*late.pop())
                    i2 = st["AT"] % 2
                    st["AT"] += 1
                    ev = AC.do(lambda e, bk=bk, i2=i2: e.activation(
                        ADJT[:, i2], banks[bk][:, :].rearrange("p (k n) -> p k n", n=P), ACT.Copy),
                        tp, at_free[i2])
                    free[bk] = ev
                    late.append((t, hf, i2, ev))
                    if hf == 0:
                        yield
                adj_free[k] = (tp, d)
                yield
            messages(*late.pop())
            yield
            result(*results.pop())
            while counts:
                count(*counts.pop(0))
                yield

        def thin(g, b, t_cum, t_nei):
            nb, u, sk, a15, hh, v = (SK[:, i, :] for i in range(6))
            mk = MK[:, (2 * g + b) * T:(2 * g + b) * T + T]
            ps = PO.do
            q = ps(lambda e: e.tensor_scalar(u, nb, 10.0, None, ALU.is_gt), t_cum[-1])
            q = ps(lambda e: e.tensor_tensor(u, u, mk, ALU.mult), q, t_mk)
            q = ps(lambda e: e.tensor_scalar(sk, nb, 0.5, 0.25, ALU.mult, ALU.add), q)
            q = ps(lambda e: e.tensor_scalar(sk, sk, 8388608.0, None, ALU.add), q)
            q = ps(lambda e: e.tensor_scalar(sk, sk, -8388608.0, None, ALU.add), q)
            q = ps(lambda e: e.tensor_scalar(v, sk, -1.5, None, ALU.mult), q)
            q = ps(lambda e: e.tensor_tensor(a15, v, u, ALU.mult), q)
            q = ps(lambda e: e.tensor_scalar(hh, sk, 0.5, -NOMATCH, ALU.mult, ALU.add), q)
            q = ps(lambda e: e.tensor_tensor(hh, hh, u, ALU.mult), q)
            q = ps(lambda e: e.tensor_scalar(hh, hh, NOMATCH, None, ALU.add), q)
            t_abs = []
            for t in range(T):
                cu = CUM[:, t * N:t * N + N]
                t_abs.append(AC.do(lambda e, cu=cu, t=t: e.activation(cu, cu, ACT.Abs,
                                                                     bias=SK[:, 3, t:t + 1]), q))
            for _ in range(LAG):
                yield
            for t in range(T):
                cu = CUM[:, t * N:t * N + N]
                w = DV.do(lambda e, cu=cu, t=t: e.tensor_scalar(cu, cu, SK[:, 4, t:t + 1], None,
                                                                ALU.is_equal), t_abs[t])
                if t % 4 == 3:
                    yield
            tok["sk_read"] = tok["rem", b] = w
            tok["nei", b] = t_nei[-1]

        def score(g, b):
            slot = (2 * g + b) % 3
            nd = POS[:, slot]
            for k in range(T):
                for ch in range(2):
                    bk = ring("T")

                    def sums(e, bk=bk, k=k, ch=ch):
                        o = banks[bk]
                        for j in range(4):
                            t = 4 * ch + j
                            oj = o[:, j * P:j * P + P]
                            at = t * N + k * P
                            e.matmul(oj, NEI[:, at:at + P], CH[:, CH_ID, :], start=(j == 0),
                                     stop=False, skip_group_check=True)
                            e.matmul(oj, CUM[:, at:at + P], CH[:, CH_NEG, :], start=False,
                                     stop=False, skip_group_check=True)
                            if t == k:
                                e.matmul(oj, CH[:, CH_ID, :], CH[:, CH_ID, :], start=False,
                                         stop=False, skip_group_check=True)
                        return e.matmul(o[:, :], CH[:, CH_NEG, :],
                                        CUM[:, k * N + 512 * ch:k * N + 512 * ch + 512],
                                        start=False, stop=True, skip_group_check=True)
                    w = PE.do(sums, tok["rem", b], tok["nei", b], free[bk])
                    ndc = nd[:, k, 512 * ch:512 * ch + 512]
                    free[bk] = AC.do(lambda e, ndc=ndc, bk=bk: e.activation(ndc, banks[bk][:, :],
                                                                          ACT.Relu), w, tok.get(("pos_read", slot)))
                if k % 2 == 1:
                    yield
            tok["nei_read"] = w
            tok["nd", b] = free[bk]

        def places(g, b):
            sl = g % 2
            nd, t_nd = POS[:, (2 * g + b) % 3], tok["nd", b]
            for ch in range(2):
                bk = ring("T")
                cs = slice(512 * ch, 512 * ch + 512)

                def total(e, bk=bk, cs=cs):
                    for k in range(T):
                        m = e.matmul(banks[bk][:, :], CH[:, CH_ONE, :], nd[:, k, cs],
                                     start=(k == 0), stop=(k == T - 1))
                    return m
                w = PE.do(total, t_nd, free[bk])
                co = COEF[:, sl, b, cs]
                t_co = free[bk] = AC.do(lambda e, co=co, bk=bk: e.activation(
                    co, banks[bk][:, :], ACT.Copy), w, tok.get(("coef_read", sl)))
                yield
            for k in reversed(range(T)):
                for ch in range(2):
                    bk = ring("T")
                    cs = slice(512 * ch, 512 * ch + 512)

                    def place(e, bk=bk, k=k, cs=cs):
                        for j in range(k + 1):
                            m = e.matmul(banks[bk][:, :], CH[:, CH_PRE if j == k else CH_ONE, :],
                                         nd[:, j, cs], start=(j == 0), stop=(j == k))
                        return m
                    w = PE.do(place, t_nd, free[bk])
                    free[bk] = AC.do(lambda e, k=k, cs=cs, bk=bk: e.activation(
                        nd[:, k, cs], banks[bk][:, :], ACT.Copy), w)
                if k % 2 == 0:
                    yield
            tok["pos", b] = free[bk]
            fl = FLO if b == 0 else FL
            for i, (n0, n1, d) in enumerate(CAPS):
                f = AC.do(lambda e, n0=n0, n1=n1, i=i: e.activation(
                    fl[:, n0:n1], COEF[0:1, sl, b, n0:n1], ACT.Relu, bias=CF[0:1, CF_CAP + i:CF_CAP + i + 1]),
                    t_co, *(tok.get("fl_read", ()) if b else (tok.get("flo_read"),)))
            if b == 0:
                tok["flo"] = f
            else:
                tok["flo_read"] = PO.do(lambda e: e.tensor_tensor(FL[:, :], FL[:, :], FLO[:, :], ALU.add), f,
                                        tok["flo"])
            for h in range(4):
                co = COEF[:, sl, b, 256 * h:256 * h + 256]
                parts = (RQ[:, 0, :], RQ[:, 1, :], co)
                for q, o in enumerate(parts):
                    r = AC.do(lambda e, q=q, o=o, co=co: e.activation(
                        o, co, ACT.Abs, scale=TAUS[q], bias=CF[:, CF_BIASQ + q:CF_BIASQ + q + 1]),
                        t_co, f, tok.get("rq_read"), *((r,) if q == 2 else ()))
                for q, o in enumerate(parts):
                    r = AC.do(lambda e, q=q, o=o: e.activation(
                        o, o, ACT.Relu, scale=-WTS[q], bias=CF[:, CF_WQ + q:CF_WQ + q + 1]),
                        *((r,) if q == 0 else ()))
                r = PO.do(lambda e, co=co: e.tensor_tensor(co, co, RQ[:, 0, :], ALU.add), r)
                r = PO.do(lambda e, co=co: e.tensor_tensor(co, co, RQ[:, 1, :], ALU.add), r)
                tok["rq_read"] = r
                if h % 2:
                    yield
            tok["coef", sl, b] = r
            tok["flags"] = tok.get("flo_read")

        def prepare_early(g):
            for _ in range(IDLE):
                yield
            first_norm(g)
            yield
            for b in range(2):
                t_cum, t_nei = [], []
                if b == 1 and g == 0:
                    yield from mix((8, places(g, 0)), (16, first_layer(g, b, t_cum, t_nei)))
                else:
                    yield from first_layer(g, b, t_cum, t_nei)
                yield from thin(g, b, t_cum, t_nei)
                if b == 0:
                    yield from score(g, 0)
                    if g > 0:
                        yield from places(g, 0)
                else:
                    second_norm(g)
                    yield

        def flags(g):
            tok["any"] = DV.do(lambda e: e.tensor_reduce(ANY[0:1, g:g + 1], FL[:, :], AX, ALU.add),
                               tok["flags"])

        def turn(g):
            for hf in range(2):
                bk = ring("T")
                for j in range(4):
                    h1 = H1[:, 4 * hf + j].rearrange("p b c -> p (b c)")
                    tp = PE.do(lambda e, bk=bk, j=j, h1=h1: e.transpose(
                        banks[bk][:, j * P:j * P + P], h1, idf), tok["h1"], free[bk] if j == 0 else None)
                free[bk] = AC.do(lambda e, bk=bk, hf=hf: e.activation(
                    H1T[:, 512 * hf:512 * hf + 512], banks[bk][:, :], ACT.Copy), tp, tok.get("h1t_read"))
            tok["h1_read"] = tp
            tok["h1t"] = free[bk]

        def overflow(g, my):
            g0, g1 = banks["G0"], banks["G1"]
            any_ap = ANY[0:1, g:g + 1].bitcast(I32)
            fl_ap = FL[0:1, :].bitcast(I32)
            room = OHB[:, :].bitcast(F32).rearrange("p (i n) -> p i n", n=N)
            va, vb, wt, io = (room[:, i, :] for i in range(4))
            u, u2 = ADJ[:, 0, :], ADJ[:, 1, :]
            slots = [(2 * g + b) % 3 for b in range(2)]

            def on_pe(e):
                flag = e.value_load(any_ap)
                with e.If(flag):
                    with e.Fori(0, N // 2) as i:
                        f = e.value_load(fl_ap[:, bass.ds(i, 1)])
                        with e.If(f):
                            for _ in range(2):
                                e.wait_ge(f_d, 1)
                                e.sem_clear(f_d)
                                for k in range(T):
                                    gb = (g0, g1)[k // 4]
                                    for b in range(2):
                                        mm = e.matmul(gb[C * b:C * b + C, (k % 4) * P:(k % 4) * P + P],
                                                      COL[:, b, k, :].to_broadcast([P, C]),
                                                      CH[:, CH_ID, :], start=(k % 4 == 0),
                                                      stop=(k % 4 == 3), skip_group_check=True)
                                mm.then_inc(f_p, 1)
                return e.sem_inc(f_e, 1)

            def on_dve(e):
                def link(ins):
                    ins.then_inc(f_l, 1)
                    e.wait_ge(f_l, 1)
                    e.sem_clear(f_l)

                flag = e.value_load(any_ap)
                with e.If(flag):
                    link(e.memset(ZF[:, :], -BIG))
                    link(e.memset(u, 1.0))
                    link(e.tensor_tensor_scan(io, u, u, 0.0, ALU.add, ALU.max))
                    with e.Fori(0, N // 2) as i:
                        f = e.value_load(fl_ap[:, bass.ds(i, 1)])
                        with e.If(f):
                            for odd in range(2):
                                for b in range(2):
                                    link(e.tensor_copy(COL[:, b], POS[:, slots[b], :, bass.ds(i * 2 + odd, 1)]))
                                e.sem_inc(f_d, 1)
                                e.wait_ge(f_p, 1)
                                e.sem_clear(f_p)
                                for j, gb in enumerate((g0, g1)):
                                    link(e.tensor_scalar(va[:, 512 * j:512 * j + 512], gb[:, :], 1024.5,
                                                         BIG, ALU.is_lt, ALU.mult))
                                link(e.tensor_scalar(u, va, 0.5 * BIG, None, ALU.is_gt))
                                link(e.tensor_reduce(FB[:, 3:4], u, AX, ALU.add))
                                link(e.tensor_scalar(FB[:, 0:1], FB[:, 3:4], -1.0, float(N), ALU.mult,
                                                     ALU.add))
                                link(e.tensor_tensor(va, va, H1T[:, :], ALU.max))
                                cur, nxt = va, vb
                                for p, k in merge_stages(N):
                                    c3 = cur.rearrange("q (n o) -> q n o", o=1)
                                    n3 = nxt.rearrange("q (n o) -> q n o", o=1)
                                    a0, a1, ar = stage_views(c3, p, k)
                                    b0, b1, br = stage_views(n3, p, k)
                                    link(e.tensor_tensor(b0, a0, a1, ALU.min))
                                    link(e.tensor_tensor(b1, a0, a1, ALU.max))
                                    if ar is not None:
                                        link(e.tensor_copy(br, ar))
                                    cur, nxt = nxt, cur
                                nv = FB[:, 0:1]
                                link(e.memset(wt, 0.0))
                                for q in range(3):
                                    link(e.tensor_scalar(FB[:, 1:2], nv, TAUS[q], 1.0 - TAUS[q],
                                                         ALU.mult, ALU.add))
                                    link(e.tensor_scalar(u, io, FB[:, 1:2], None, ALU.subtract))
                                    link(e.tensor_scalar(u2, u, -1.0, None, ALU.mult))
                                    link(e.tensor_tensor(u, u, u2, ALU.min))
                                    link(e.tensor_scalar(u, u, 1.0, 0.0, ALU.add, ALU.max))
                                    link(e.scalar_tensor_tensor(out=wt, in0=u, scalar=WTS[q], in1=wt,
                                                                op0=ALU.mult, op1=ALU.add))
                                link(e.tensor_tensor(nxt, cur, wt, ALU.mult))
                                link(e.tensor_reduce(FB[:, 2:3], nxt, AX, ALU.add))
                                link(e.tensor_tensor(ZF[:, bass.ds(i * 2 + odd, 1)], FB[:, 2:3],
                                                     H1T[:, bass.ds(i * 2 + odd, 1)], ALU.add))
                return e.memset(MARK[:, :], 0.0)

            PE.do(on_pe, tok["any"], tok["pos", 0], tok["pos", 1], free["G0"], free["G1"], c_all)
            tok["mark"] = DV.do(on_dve, tok["any"], tok["h1t"], tok.get("mark"), tok["oh_last"],
                                *adj_free[0], *adj_free[1])
            tok["fl_read"] = (tok["mark"], DmaToken(f_e, g + 1))
            free["G0"] = free["G1"] = oh_free[0] = oh_free[1] = tok["mark"]
            for i in slots:
                tok["pos_read", i] = tok["mark"]
            for i in range(NADJ):
                adj_free[i] = (*adj_free[i], tok["mark"])

        def chunks_of(ci, cols, lane0=0):
            n0, n1, d = CLASSES[ci]
            w = n1 - n0
            if ci == 0:
                return [(0, HUB_LANES, j, 32) for j in range(0, 64, 32)]
            if ci == 3:
                w = THIRD
            per = cols // w
            return [(lane0, w, j, min(per, d - j)) for j in range(0, d, per)]

        class Half:
            pass

        def gather(ci, lane0, w, d0, nd, half, bk, my):
            n0 = CLASSES[ci][0] + lane0
            c = Half()
            c.bk, c.cols = bk, w * nd
            r = st["OH"] = (st.get("OH", -1) + 1) % 2
            ohs = []
            for b in range(2):
                oh = OHB[:, (2 * r + b) * 4 * COLS:(2 * r + b) * 4 * COLS + 4 * c.cols]\
                    .rearrange("p (k c) -> p k c", k=4)
                ps = POS[:, my["pos"][b], 4 * half:4 * half + 4, n0:n0 + w]
                waits = (tok["pos", b], oh_free[r])
                if ci == 0:
                    ps = HUB[:, b, 4 * half:4 * half + 4, :]
                    waits = (tok["hub", b], oh_free[r])
                    ov = oh.rearrange("p k (d n) -> p k d n", n=w)
                    pv = ps.unsqueeze(2).to_broadcast([P, 4, nd, w])
                    iv = CH[:, CH_IOTA, d0:d0 + nd].unsqueeze(1).unsqueeze(3).to_broadcast([P, 4, nd, w])
                    for kk in range(4):
                        t = DV.do(lambda e, ov=ov, pv=pv, iv=iv, kk=kk: e.tensor_tensor(
                            ov[:, kk], pv[:, kk], iv[:, kk], ALU.is_equal), *waits, c_all)
                else:
                    for j in range(nd):
                        t = DV.do(lambda e, oh=oh, ps=ps, j=j, d=d0 + j, w=w: e.tensor_scalar(
                            oh[:, :, j * w:j * w + w], ps, float(N + 1 + d), None, ALU.is_equal), *waits)
                ohs.append(oh)

            def mms(e):
                for kk in range(4):
                    k = 4 * half + kk
                    for part in range(2):
                        for b in range(2):
                            m = e.matmul(banks[bk][C * b:C * b + C, 0:c.cols], HL[:, part, b, k, :],
                                         ohs[b][:, kk, :], start=(k == 0 and part == 0),
                                         stop=(k == T - 1 and part == 1), skip_group_check=True)
                return m

            def matmuls():
                c.mm = oh_free[r] = tok["oh_last"] = PE.do(mms, t, tok["hl"], free[bk])

            c.matmuls = matmuls
            if ci == 0:
                tok["hub_read"] = t
            return c

        def hubs(g, my):
            for b in range(2):
                ps, w = POS[:, my["pos"][b]], (tok["pos", b], tok.get("hub_read"))
                PO.do(lambda e, b=b, ps=ps: e.tensor_copy(HUB[:, b, :, 0:HUBS], ps[:, :, 0:HUBS]), *w)
                PO.do(lambda e, b=b, ps=ps: e.tensor_scalar(
                    HUB[:, b, :, HUBS:2 * HUBS], ps[:, :, 0:HUBS], -64.0, None, ALU.add), *w)
                tok["hub", b] = PO.do(lambda e, b=b, ps=ps: e.tensor_copy(
                    HUB[:, b, :, 2 * HUBS:], ps[:, :, HUBS:8]), *w)

        def gather_all(ci, buf, my, *waits, lane0=0):
            def copy(c):
                if c.dst is not None:
                    free[c.bk] = AC.do(lambda e: e.activation(c.dst, banks[c.bk][:, 0:c.cols], ACT.Copy),
                                       c.mm, *waits)
                return free[c.bk]

            to_mul, to_copy = [], []
            for a in chunks_of(ci, COLS, lane0):
                bk = ring("G")
                for half in range(2):
                    c = gather(ci, *a, half, bk, my)
                    c.dst = buf[:, a[2] * a[1]:a[2] * a[1] + c.cols] if half else None
                    if to_copy:
                        copy(to_copy.pop())
                    if to_mul:
                        to_mul[0].matmuls()
                        to_copy.append(to_mul.pop())
                    to_mul.append(c)
                    yield
            if to_copy:
                copy(to_copy.pop())
            to_mul[0].matmuls()
            my["ev", ci] = copy(to_mul[0])

        def batcher(ci, my):
            n0, n1, d = CLASSES[ci]
            w = n1 - n0
            if ci == 0:
                w, d = HUB_LANES, 64
            cur, nxt = (v[:, 0:d * w].rearrange("p (d n) -> p d n", n=w) for v in (SZ if ci == 0 else SA, SB))
            t = my["ev", ci]
            for p, k in merge_stages(d):
                a0, a1, ar = stage_views(cur, p, k)
                b0, b1, br = stage_views(nxt, p, k)
                wb = (t, tok.get("sb_read"))
                t = DV.do(lambda e, b0=b0, a0=a0, a1=a1: e.tensor_tensor(b0, a0, a1, ALU.max), *wb)
                t = DV.do(lambda e, b1=b1, a0=a0, a1=a1: e.tensor_tensor(b1, a0, a1, ALU.min), *wb)
                if ar is not None:
                    t = DV.do(lambda e, br=br, ar=ar: e.tensor_copy(br, ar), *wb)
                cur, nxt = nxt, cur
                yield
            if ci == 0:
                lanes = cur
                m0, m1 = (v.rearrange("p (d n) -> p d n", n=HUBS)
                          for v in (SZ[:, 640:640 + 128 * HUBS], SB[:, 1024:1024 + 128 * HUBS]))
                low, high = lanes[:, :, 0:HUBS], lanes[:, :, HUBS:2 * HUBS]
                w = t
                DV.do(lambda e: e.tensor_tensor(m0[:, 0:64, :], low, high, ALU.max), w)
                t = DV.do(lambda e: e.tensor_tensor(m0[:, 64:128, :], low, high, ALU.min), w)
                for p, k in list(merge_stages(128))[-6:]:
                    a0, a1, ar = stage_views(m0, p, k)
                    b0, b1, br = stage_views(m1, p, k)
                    w = t
                    DV.do(lambda e, b0=b0, a0=a0, a1=a1: e.tensor_tensor(b0, a0, a1, ALU.max), w)
                    DV.do(lambda e, b1=b1, a0=a0, a1=a1: e.tensor_tensor(b1, a0, a1, ALU.min), w)
                    t = DV.do(lambda e, br=br, ar=ar: e.tensor_copy(br, ar), w)
                    m0, m1 = m1, m0
                    yield
                cur = (m0, lanes[:, :, 2 * HUBS:])
            tok["sb_read"] = t
            my["sorted", ci] = (cur, t)

        def coef_rows(my, ci, lane0, w, d0, nd):
            n0 = CLASSES[ci][0] + lane0
            bk = ring("S")
            co = COEF[:, my["sl"]]

            def mms(e):
                oo = [banks[bk][C * b:C * b + C, 0:w * nd] for b in range(2)]
                if ci == 0:
                    ov = [o.rearrange("p (d n) -> p d n", n=w) for o in oo]
                    for n in range(w):
                        for b in range(2):
                            m = e.matmul(ov[b][:, :, n], co[:, b, n0 + n:n0 + n + 1].to_broadcast([P, C]),
                                         CH[:, CH_SEL, d0:d0 + nd], start=(n == 0), stop=(n == w - 1),
                                         skip_group_check=True)
                else:
                    for j in range(nd):
                        for b in range(2):
                            m = e.matmul(oo[b][:, j * w:j * w + w],
                                         CH[:, CH_SEL, d0 + j:d0 + j + 1].to_broadcast([P, C]),
                                         co[:, b, n0:n0 + w], start=(j == 0), stop=(j == nd - 1),
                                         skip_group_check=True)
                return m
            t = PE.do(mms, tok["coef", my["sl"], 0], tok["coef", my["sl"], 1], free[bk], c_all)
            tok["coef_read", my["sl"]] = t
            return bk, t

        def first_rows(my, ci, chunks):
            my["rows", ci, chunks[0]] = coef_rows(my, ci, *chunks[0])

        def ahead(my, ci, chunks):
            got = my.pop(("rows", ci, chunks[0]), None) or coef_rows(my, ci, *chunks[0])
            for a, after in itertools.zip_longest(chunks, chunks[1:]):
                now, got = got, after and coef_rows(my, ci, *after)
                yield a, now

        def weigh(ci, my):
            n0, n1, d = CLASSES[ci]
            w = n1 - n0
            cur, t = my["sorted", ci]
            if ci == 0:
                sorted_ = t
                for v, ((l0, w, d0, nd), (bk, mm)) in zip(cur, ahead(my, 0, HUB_PARTS)):
                    t = free[bk] = DV.do(lambda e, v=v, bk=bk, w=w, nd=nd: e.tensor_tensor(
                        v, v, banks[bk][:, 0:nd * w].rearrange("p (d n) -> p d n", n=w), ALU.mult),
                        sorted_, mm)
                    yield
                for v, lo, hi in zip(cur, (0, HUBS), (HUBS, 8)):
                    r = DV.do(lambda e, v=v, lo=lo, hi=hi: e.tensor_reduce(
                        RED[:, lo:hi], v.rearrange("p d n -> p n d"), AX, ALU.add), t, tok.get("red_read"))
                tok["sz_read"] = tok["sb_read"] = my["red", 0] = r
                yield
                return
            flat = cur.rearrange("p d n -> p (d n)")
            for (lane0, w_, d0, nd), (bk, mm) in ahead(my, ci, chunks_of(ci, 512)):
                v = flat[:, d0 * w:(d0 + nd) * w]
                t = DV.do(lambda e, v=v, bk=bk, n=nd * w: e.tensor_tensor(v, v, banks[bk][:, 0:n], ALU.mult),
                          t, mm)
                free[bk] = t
                yield
            r = DV.do(lambda e: e.tensor_reduce(RED[:, n0:n1], cur.rearrange("p d n -> p n d"), AX, ALU.add),
                      t, tok.get("red_read"))
            tok["sa_read"] = r
            if ci == 1:
                tok["sb_read"] = r
            my["red", ci] = r
            yield

        def network(my):
            loc = list(range(11))
            spare = [(i, tok.get("sl_read")) for i in range(11, NSL)]
            layer = my["ev", 3]
            for level in NET11:
                t = None
                for i, j in level:
                    (la, lb) = loc[i], loc[j]
                    (s1, r1), (s2, r2) = spare.pop(0), spare.pop(0)
                    DV.do(lambda e, la=la, lb=lb, s1=s1: e.tensor_tensor(SL[:, s1, :], SL[:, la, :],
                                                                        SL[:, lb, :], ALU.max), layer, r1)
                    t = DV.do(lambda e, la=la, lb=lb, s2=s2: e.tensor_tensor(SL[:, s2, :], SL[:, la, :],
                                                                            SL[:, lb, :], ALU.min), layer, r2)
                    loc[i], loc[j] = s1, s2
                    spare += [(la, t), (lb, t)]
                    yield
                layer = t
            my["sorted", 3] = (loc, layer)

        def weigh_last(my, lane0):
            loc, t_sorted = my["sorted", 3]
            for (l0, w, d0, nd), (bk, mm) in ahead(my, 3, chunks_of(3, 512, lane0)):
                for j in range(nd):
                    d = d0 + j
                    v = SL[:, loc[d], :]
                    t = DV.do(lambda e, v=v, bk=bk, j=j, w=w: e.tensor_tensor(
                        v, v, banks[bk][:, j * w:j * w + w], ALU.mult), t_sorted, mm)
                    s_ = PE.do(lambda e, v=v, d=d, w=w: e.matmul(
                        banks["M"][:, 0:w], idf, v, start=(d == 0), stop=(d == 10)), t,
                        free["M"] if d == 0 else None)
                free[bk] = t
                yield
            tok["sl_read"] = s_
            yield
            n = CLASSES[3][0] + lane0
            t = free["M"] = DV.do(lambda e, n=n: e.tensor_tensor(
                Z[:, n:n + THIRD], banks["M"][:, 0:THIRD], H1T[:, n:n + THIRD], ALU.add), s_, tok["h1t"],
                tok.get("z_read"))
            my["z", lane0] = t
            yield

        def last_third(my, lane0):
            for i, _ in enumerate(network(my)):
                if i == 34 - PRE:
                    first_rows(my, 3, chunks_of(3, 512, lane0))
                yield
            yield from weigh_last(my, lane0)

        def agree(g, my):
            t = DV.do(lambda e: e.tensor_tensor(Z[:, 0:256], RED[:, :], H1T[:, 0:256], ALU.add),
                      my["red", 0], my["red", 1], my["red", 2], tok["h1t"], tok.get("z_read"))
            tok["red_read"] = t
            any_ap = ANY[0:1, g:g + 1].bitcast(I32)

            def patch(e):
                def link(ins):
                    ins.then_inc(f_l, 1)
                    e.wait_ge(f_l, 1)
                    e.sem_clear(f_l)

                flag = e.value_load(any_ap)
                with e.If(flag):
                    for ch in range(2):
                        mask = SB[:, 0:512].bitcast(I32)
                        zf, zc = (v[:, 512 * ch:512 * ch + 512] for v in (ZF, Z))
                        link(e.tensor_scalar(mask, zf, -0.5 * BIG, None, ALU.is_gt))
                        link(e.copy_predicated(zc, mask, zf))
                return e.memset(MARK[:, :], 0.0)
            t = tok["mark"] = DV.do(patch, t, *(my["z", i * THIRD] for i in range(3)), tok["mark"],
                                    tok.get("sb_read"))
            tok["h1t_read"] = my["z"] = tok["sb_read"] = t

        def finish(g, my):
            sl = g % 3
            t_z = my["z"]
            hid = [SZ[:, 0:512], SZ[:, 512:1024]]
            tmp = SB[:, 0:512]
            added = []
            hr = [None, None]
            for b in range(2):
                bm = "M"
                for ch in range(2):
                    bk = ring("T")
                    w = PE.do(lambda e, b=b, ch=ch, bk=bk: e.matmul(
                        banks[bk][:, :], W1[C * b:C * b + C, :], Z[C * b:C * b + C, 512 * ch:512 * ch + 512], start=True,
                        stop=True), t_z, free[bk])
                    a = AC.do(lambda e, bk=bk, ch=ch: e.activation(hid[ch], banks[bk][:, :], ACT.Relu,
                                                                  bias=B1[:, 0:1]), w, hr[ch], tok["sz_read"])
                    free[bk] = a
                    tok["z_read"] = w

                    def second(e, ch=ch, bm=bm):
                        for j in range(4):
                            o = banks[bm][:, (4 * ch + j) * C:(4 * ch + j) * C + C]
                            e.matmul(o, hid[ch][:, j * P:j * P + P], W2[:, :], start=(ch == 0 and j == 0),
                                     stop=False, skip_group_check=True)
                            m = e.matmul(o, CF[0:1, CF_ONE:CF_ONE + P], B2[0:1, :], start=False,
                                         stop=(ch == 1 and j == 3), skip_group_check=True)
                        return m
                    y = PE.do(second, a, free[bm])
                    hr[ch] = y
                for _ in range(REST):
                    yield
                mk = MK[:, (2 * g + b) * T:(2 * g + b) * T + T].unsqueeze(2).to_broadcast([P, T, C])
                tv = tmp.rearrange("p (t c) -> p t c", c=C)
                t = DV.do(lambda e, tv=tv, mk=mk, bm=bm: e.tensor_tensor(
                    tv, banks[bm][:, :].rearrange("p (t c) -> p t c", c=C), mk, ALU.mult), y,
                    tok["sb_read"], t_z)
                free[bm] = t
                xv = X[:, sl, b]
                t = PO.do(lambda e, tv=tv, xv=xv: e.tensor_tensor(xv, xv, tv, ALU.add), t)
                tok["sb_read"] = t
                added.append(t)
                yield
            tok["sz_read"] = y
            yield from pause(STORE)
            for b in range(2):
                out_n[sl] += 16
                x_free[sl] = dma(out_d[2 * g + b].rearrange("(t p) c -> p t c", p=P), X[:, sl, b], s_out[sl],
                                 out_n[sl], added[b])
            yield from pause(STORE)

        def mix(*gens):
            total = max(n for n, _ in gens)
            done = [0] * len(gens)
            for i in range(total):
                for j, (n, gen) in enumerate(gens):
                    while done[j] * total < (i + 1) * n:
                        next(gen, None)
                        done[j] += 1
                yield
            for _, gen in gens:
                yield from gen

        def chain(*gens):
            for gen in gens:
                yield from gen

        def run(gen):
            for _ in gen:
                pass

        def pause(n):
            for _ in range(n):
                yield

        def sort_and_weigh(ci, my):
            for i, _ in enumerate(batcher(ci, my)):
                if i == (21 if ci == 0 else 10):
                    first_rows(my, ci, HUB_PARTS if ci == 0 else chunks_of(ci, 512))
                yield
            yield from weigh(ci, my)

        def third(my, i):
            yield from gather_all(3, SL[:, :, :].rearrange("p s n -> p (s n)"), my, tok.get("sl_read"),
                                  lane0=i * THIRD)

        def class_(ci, my):
            buf, read = (SZ, "sz_read") if ci == 0 else (SA, "sa_read")
            yield from gather_all(ci, buf, my, tok.get(read))

        def finish_and_load(g, my):
            yield from finish(g, my)
            if g + 3 < NP:
                load_x(g + 3)

        load_x(0)
        load_x(1)
        load_x(2)
        run(prepare_early(0))
        run(score(0, 1))
        halves(0)
        run(places(0, 1))
        flags(0)
        turn(0)
        def close(g, my):
            yield from sort_and_weigh(0, my)
            agree(g, my)
            yield
            if g + 1 < NP:
                turn(g + 1)
                yield

        sums, results = iter(()), iter(())
        for g in range(NP):
            my = {"sl": g % 2, "pos": [(2 * g + b) % 3 for b in range(2)]}
            third_sort = batcher(2, my)
            hubs(g, my)
            gathers = chain(
                mix((12, third(my, 0)), (33, sums)),
                mix((12, class_(1, my)), (42 + PAUSE, chain(pause(PAUSE), last_third(my, 0))), (42, results)),
                mix((12, third(my, 1)), (22 + PAUSE // 2, chain(pause(PAUSE // 2), sort_and_weigh(1, my)))),
                mix((12, class_(2, my)), (42 + PAUSE, chain(pause(PAUSE), last_third(my, THIRD)))),
                class_(0, my),
                mix((12, third(my, 2)), (12, itertools.islice(third_sort, SPLIT if g + 1 < NP else 12))))
            if g + 1 < NP:
                run(mix((33 + 42 + 22 + 42 + 16 + 5 * PAUSE // 2, gathers), (EARLY, prepare_early(g + 1))))
            else:
                run(gathers)
            tok["oh_read"] = tok["oh_last"]
            overflow(g, my)
            if g + 1 < NP:
                halves(g + 1)
                run(score(g + 1, 1))
                run(places(g + 1, 1))
            run(third_sort)
            run(last_third(my, 2 * THIRD))
            run(weigh(2, my))
            if g + 1 < NP:
                flags(g + 1)
            sums, results = close(g, my), finish_and_load(g, my)
        run(sums)
        run(results)

        for lane in (PE, AC, DV, PO, SP):
            lane.count()
        block = ctx.enter_context(nc.Block())

        @block.tensor
        def _(e):
            PE.issue(e)

        @block.scalar
        def _(e):
            AC.issue(e)

        @block.vector
        def _(e):
            DV.issue(e)

        @block.gpsimd
        def _(e):
            PO.issue(e)

        @block.sync
        def _(e):
            SP.issue(e)
            for i in range(3):
                e.wait_ge(s_out[i], out_n[i])


def constants():
    import numpy as np

    cf = np.zeros((P, CF_N), np.float32)
    cf[:, CF_ID:CF_ID + P] = np.eye(P)
    d = np.arange(P)
    for q in range(3):
        cf[:, CF_BIASQ + q] = -(TAUS[q] + d)
        cf[:, CF_WQ + q] = WTS[q]
    cf[:, CF_EPS] = 1e-5
    for i, (_, _, slots) in enumerate(CAPS):
        cf[:, CF_CAP + i] = -slots
    cf[:, CF_ONE:CF_ONE + P] = 1.0
    ch = np.zeros((P, 7, P), np.float16)
    ch[:, CH_ID] = np.eye(P)
    ch[:, CH_NEG] = -np.eye(P)
    ch[:, CH_PRE] = np.triu(np.ones((P, P))) + N * np.eye(P)
    ch[:, CH_ONE] = 1.0
    ch[:, CH_OFF] = 1.0 - np.eye(P)
    ch[:, CH_IOTA] = N + 1 + d[None, :]
    ch[:, CH_SEL] = np.eye(P) / HSCALE
    return cf, ch


def kernel(x, adj, nodemask, L1_gnn_W1, L1_gnn_b1, L1_gnn_W2, L1_gnn_b2):
    import numpy as np
    import concourse.bacc as bacc
    from concourse.bass_utils import run_bass_kernel_spmd

    nc = bacc.Bacc("TRN2", target_bir_lowering=False, num_devices=1)
    cf, ch = constants()
    given = {
        "x": x, "adj": adj, "nodemask": np.ascontiguousarray(nodemask).view(np.uint8), "w1": L1_gnn_W1,
        "b1": L1_gnn_b1, "w2": L1_gnn_W2, "b2": L1_gnn_b2, "cf": cf, "ch": ch,
    }
    arrays, args = {}, []
    for name, a in given.items():
        a = np.ascontiguousarray(a)
        arrays[f"in_{name}"] = a
        args.append(nc.dram_tensor(f"in_{name}", a.shape, mybir.dt.from_np(a.dtype),
                                   kind="ExternalInput").ap())
    out = nc.dram_tensor("out_0", (B, N, C), F32, kind="ExternalOutput").ap()
    program(nc, *args, out)
    r = run_bass_kernel_spmd(nc, [arrays], core_ids=[0])
    return r.results[0]["out_0"]
```
